# Optimizing a Trainium2 kernel written in Bass

```python
import numpy as np
import jax
import jax.numpy as jnp

def _softmax(x, axis=-1):
    return jax.nn.softmax(x, axis=axis)

def _gelu(x):
    return jax.nn.gelu(x, approximate=True)

def _silu(x):
    return jax.nn.silu(x)

def _sigmoid(x):
    return jax.nn.sigmoid(x)

def _layernorm(x, axis=-1, eps=1e-05):
    m = jnp.mean(x, axis=axis, keepdims=True)
    v = jnp.var(x, axis=axis, keepdims=True)
    return (x - m) / jnp.sqrt(v + eps)

def _scatter_add(tgt, idx, src, axis=0):
    return tgt.at[idx].add(src)

def _segment_sum(src, seg, n):
    return jax.ops.segment_sum(src, seg, n)
kernel_name = 'mk_adj_preln_d4_adj_r2_2029e1'

def setup_inputs(seed: int=0):
    np.random.seed(seed)
    _w = jnp.asarray

    def _rec_inputs():
        import jax
        import jax.numpy as jnp
        _gk = jax.random.key(seed)
        x = -0.0002928 + 1 * jax.random.normal(jax.random.fold_in(_gk, 1), (128, 128, 256), jnp.float32)
        _a = jax.random.bernoulli(jax.random.fold_in(_gk, 2), 0.0625, (128, 128, 128))
        _a = jnp.logical_or(_a, jnp.swapaxes(_a, -1, -2))
        _a = jnp.logical_or(_a, jnp.eye(128, dtype=bool))
        _af = _a.astype(jnp.float32)
        _af = _af * jax.random.uniform(jax.random.fold_in(_gk, 3), (128, 128, 128), jnp.float32, 0.05, 1)
        adj = _af
        _nm = jnp.ones((128, 128), dtype=bool)
        nodemask = _nm
        return (x, adj, nodemask)
    x, adj, nodemask = _rec_inputs()

    def _L0_gnn_setup():
        import jax, jax.numpy as jnp
        import numpy as np
        B, N, DIN, DOUT, K = (4, 1024, 256, 256, 3)
        key = jax.random.key(seed)
        ks = jax.random.split(key, 8)
        X = jax.random.normal(ks[0], (B, N, DIN), dtype=jnp.float32)
        A = jax.random.uniform(ks[1], (B, N, N), dtype=jnp.float32)
        Wv = jax.random.normal(ks[2], (DIN, DOUT), dtype=jnp.float32) * 0.02
        bv = jax.random.normal(ks[3], (DOUT,), dtype=jnp.float32) * 0.02
        aw = jax.random.normal(ks[4], (2 * DOUT, 1), dtype=jnp.float32) * 0.05
        ab = jax.random.normal(ks[5], (1,), dtype=jnp.float32) * 0.05
        Wk = jax.random.normal(ks[6], (K, DIN, DOUT), dtype=jnp.float32) * 0.02
        bk = jax.random.normal(ks[7], (K, DOUT), dtype=jnp.float32) * 0.02
        return {'X': X, 'A': A, 'Wv': Wv, 'bv': bv, 'aw': aw, 'ab': ab, 'Wk': Wk, 'bk': bk}
    _L0_gnn_all = _L0_gnn_setup()
    _L0_gnn_in = {k: v for k, v in _L0_gnn_all.items() if k in ('Wv', 'bv', 'aw', 'ab', 'Wk', 'bk')}
    del _L0_gnn_all

    def _L1_gnn_setup():
        import jax, jax.numpy as jnp
        import numpy as np
        IN_F = 256
        OUT_F = 256
        ALPHA = 0.2
        NEG_INF = -9000000000000000.0
        key = jax.random.key(seed)
        k1, k2, k3, k4 = jax.random.split(key, 4)
        B, S = (8, 1024)
        hidden_state = jax.random.normal(k1, (B, S, IN_F), dtype=jnp.float32)
        adjacent_matrix = jax.random.uniform(k2, (B, S, S), dtype=jnp.float32)
        bound = 1.0 / np.sqrt(IN_F)
        W = jax.random.uniform(k3, (IN_F, OUT_F), dtype=jnp.float32, minval=-bound, maxval=bound)
        a_bound = 1.414 * np.sqrt(6.0 / (2 * OUT_F + 1))
        a = jax.random.uniform(k4, (2 * OUT_F, 1), dtype=jnp.float32, minval=-a_bound, maxval=a_bound)
        return {'hidden_state': hidden_state, 'adjacent_matrix': adjacent_matrix, 'W': W, 'a': a}
    _L1_gnn_all = _L1_gnn_setup()
    _L1_gnn_in = {k: v for k, v in _L1_gnn_all.items() if k in ('W', 'a')}
    del _L1_gnn_all

    def _L2_gnn_setup():
        import jax, jax.numpy as jnp
        import numpy as np
        B, N, F_IN, F_HID, F_OUT = (32, 512, 256, 256, 256)

        def _gcn_layer(x, adj, W, b):
            support = jnp.einsum('bnf,fh->bnh', x, W)
            return jnp.einsum('bnm,bmh->bnh', adj, support) + b
        key = jax.random.key(seed)
        ks = jax.random.split(key, 8)

        def xavier(k, fan_in, fan_out):
            bound = float(np.sqrt(6.0 / (fan_in + fan_out)))
            return jax.random.uniform(k, (fan_in, fan_out), jnp.float32, -bound, bound)
        return {'batch_graph': jax.random.normal(ks[0], (B, N, F_IN), jnp.float32), 'adj': jax.random.uniform(ks[1], (B, N, N), jnp.float32), 'W1': xavier(ks[2], F_IN, F_HID), 'b1': jnp.zeros((F_HID,), jnp.float32), 'W2': xavier(ks[3], F_HID, F_HID), 'b2': jnp.zeros((F_HID,), jnp.float32), 'W3': xavier(ks[4], F_HID, F_OUT), 'b3': jnp.zeros((F_OUT,), jnp.float32)}
    _L2_gnn_all = _L2_gnn_setup()
    _L2_gnn_in = {k: v for k, v in _L2_gnn_all.items() if k in ('W1', 'b1', 'W2', 'b2', 'W3', 'b3')}
    del _L2_gnn_all

    def _L3_gnn_setup():
        import jax, jax.numpy as jnp
        import numpy as np
        HEADS = 8
        DIM_HEAD = 64
        LA = 0.33
        LD = 0.33
        LG = 0.33
        key = jax.random.key(seed)
        ks = jax.random.split(key, 6)
        B, N, D = (4, 512, 256)
        inner = HEADS * DIM_HEAD
        x = jax.random.normal(ks[0], (B, N, D), jnp.float32)
        mask = jax.random.uniform(ks[1], (B, N)) < 0.9
        adjacency_mat = (jax.random.uniform(ks[2], (B, N, N)) < 0.05).astype(jnp.float32)
        distance_mat = jax.random.uniform(ks[3], (B, N, N), jnp.float32) * 5.0
        W_qkv = jax.random.normal(ks[4], (D, inner * 3), jnp.float32) * 0.02
        W_out = jax.random.normal(ks[5], (inner, D), jnp.float32) * 0.02
        b_out = jnp.zeros((D,), jnp.float32)
        return {'x': x, 'mask': mask, 'adjacency_mat': adjacency_mat, 'distance_mat': distance_mat, 'W_qkv': W_qkv, 'W_out': W_out, 'b_out': b_out}
    _L3_gnn_all = _L3_gnn_setup()
    _L3_gnn_in = {k: v for k, v in _L3_gnn_all.items() if k in ('W_qkv', 'W_out', 'b_out')}
    del _L3_gnn_all
    return {'x': x, 'adj': adj, 'nodemask': nodemask, 'L0_gnn_Wv': _L0_gnn_in['Wv'], 'L0_gnn_bv': _L0_gnn_in['bv'], 'L0_gnn_aw': _L0_gnn_in['aw'], 'L0_gnn_ab': _L0_gnn_in['ab'], 'L0_gnn_Wk': _L0_gnn_in['Wk'], 'L0_gnn_bk': _L0_gnn_in['bk'], 'L1_gnn_W': _L1_gnn_in['W'], 'L1_gnn_a': _L1_gnn_in['a'], 'L2_gnn_W1': _L2_gnn_in['W1'], 'L2_gnn_b1': _L2_gnn_in['b1'], 'L2_gnn_W2': _L2_gnn_in['W2'], 'L2_gnn_b2': _L2_gnn_in['b2'], 'L2_gnn_W3': _L2_gnn_in['W3'], 'L2_gnn_b3': _L2_gnn_in['b3'], 'L3_gnn_W_qkv': _L3_gnn_in['W_qkv'], 'L3_gnn_W_out': _L3_gnn_in['W_out'], 'L3_gnn_b_out': _L3_gnn_in['b_out']}

def reference(x, adj, nodemask, L0_gnn_Wv, L0_gnn_bv, L0_gnn_aw, L0_gnn_ab, L0_gnn_Wk, L0_gnn_bk, L1_gnn_W, L1_gnn_a, L2_gnn_W1, L2_gnn_b1, L2_gnn_W2, L2_gnn_b2, L2_gnn_W3, L2_gnn_b3, L3_gnn_W_qkv, L3_gnn_W_out, L3_gnn_b_out):
    import jax
    import jax.numpy as jnp

    def _L0_gnn_ref(X, A, Wv, bv, aw, ab, Wk, bk):
        import jax, jax.numpy as jnp
        import numpy as np
        B, N, DIN, DOUT, K = (4, 1024, 256, 256, 3)
        d = Wv.shape[1]
        Xw = X @ Wv + bv
        sj = Xw @ aw[:d, 0]
        si = Xw @ aw[d:, 0]
        e = jax.nn.leaky_relu(sj[:, None, :] + si[:, :, None] + ab[0], negative_slope=0.2)
        alpha_matrix = A * jnp.exp(e)
        transition = alpha_matrix / (jnp.sum(alpha_matrix, axis=-1, keepdims=True) + 1e-12)
        H = jnp.zeros(X.shape[:-1] + (d,), dtype=X.dtype)
        Xk = X
        for k in range(Wk.shape[0]):
            H = H + Xk @ Wk[k] + bk[k]
            Xk = jnp.einsum('bij,bjd->bid', transition, Xk)
        return jax.nn.relu(H)

    def _L1_gnn_ref(hidden_state, adjacent_matrix, W, a):
        import jax, jax.numpy as jnp
        import numpy as np
        IN_F = 256
        OUT_F = 256
        ALPHA = 0.2
        NEG_INF = -9000000000000000.0
        Wh = jnp.einsum('bsi,io->bso', hidden_state, W)
        Wh1 = Wh @ a[:OUT_F, :]
        Wh2 = Wh @ a[OUT_F:, :]
        e = Wh1 + jnp.swapaxes(Wh2, 1, 2)
        e = jax.nn.leaky_relu(e, negative_slope=ALPHA)
        attention = jnp.where(adjacent_matrix > 0.5, e, NEG_INF)
        attention = jax.nn.softmax(attention, axis=1)
        h_prime = jnp.einsum('bst,bto->bso', attention, Wh)
        return jax.nn.elu(h_prime)

    def _L2_gnn_ref(batch_graph, adj, W1, b1, W2, b2, W3, b3):
        import jax, jax.numpy as jnp
        import numpy as np
        B, N, F_IN, F_HID, F_OUT = (32, 512, 256, 256, 256)

        def _gcn_layer(x, adj, W, b):
            support = jnp.einsum('bnf,fh->bnh', x, W)
            return jnp.einsum('bnm,bmh->bnh', adj, support) + b
        x = jax.nn.relu(_gcn_layer(batch_graph, adj, W1, b1))
        x = jax.nn.relu(_gcn_layer(x, adj, W2, b2))
        out = _gcn_layer(x, adj, W3, b3)
        return out

    def _L3_gnn_ref(x, mask, adjacency_mat, distance_mat, W_qkv, W_out, b_out):
        import jax, jax.numpy as jnp
        import numpy as np
        HEADS = 8
        DIM_HEAD = 64
        LA = 0.33
        LD = 0.33
        LG = 0.33
        B, N, _ = x.shape
        scale = DIM_HEAD ** (-0.5)
        qkv = (x @ W_qkv).reshape(B, N, HEADS, 3, DIM_HEAD)
        q, k, v = (jnp.transpose(qkv[..., i, :], (0, 2, 1, 3)) for i in range(3))
        dots = jnp.einsum('bhid,bhjd->bhij', q, k) * scale
        big = jnp.finfo(dots.dtype).max
        m2 = mask[:, None, :, None] & mask[:, None, None, :]
        dots = jnp.where(m2, dots, -big)
        attn = jax.nn.softmax(dots, axis=-1) * LA
        adj = jnp.where(m2, adjacency_mat[:, None], 0.0)
        dist = jnp.where(m2, distance_mat[:, None], big)
        attn = attn + LG * adj + LD * jnp.exp(-dist)
        out = jnp.einsum('bhij,bhjd->bhid', attn, v)
        out = jnp.transpose(out, (0, 2, 1, 3)).reshape(B, N, HEADS * DIM_HEAD)
        return out @ W_out + b_out
    h = jnp.maximum(_layernorm(x, axis=-1), 0.0)
    x = x + _L0_gnn_ref(h, adj, L0_gnn_Wv, L0_gnn_bv, L0_gnn_aw, L0_gnn_ab, L0_gnn_Wk, L0_gnn_bk)
    h = jnp.maximum(_layernorm(x, axis=-1), 0.0)
    x = x + _L1_gnn_ref(h, adj, L1_gnn_W, L1_gnn_a)
    h = jnp.maximum(_layernorm(x, axis=-1), 0.0)
    x = x + _L2_gnn_ref(h, adj, L2_gnn_W1, L2_gnn_b1, L2_gnn_W2, L2_gnn_b2, L2_gnn_W3, L2_gnn_b3)
    h = jnp.maximum(_layernorm(x, axis=-1), 0.0)
    x = x + _L3_gnn_ref(h, nodemask, adj, adj, L3_gnn_W_qkv, L3_gnn_W_out, L3_gnn_b_out)
    return x

_drawn_inputs = setup_inputs


def setup_inputs(seed=0):
    import zlib

    import numpy as np

    out = dict(_drawn_inputs(seed))
    spreads = {'L2_gnn_b1': (0.0, 0.31),
     'L2_gnn_b2': (0.0, 0.8),
     'L2_gnn_b3': (0.0, 2.0),
     'L3_gnn_b_out': (0.0, 2.0)}
    factors = {'L0_gnn_Wv': 8.0, 'L0_gnn_bv': 64.0, 'L0_gnn_aw': 8.0, 'L1_gnn_a': 6.524}
    for name, (base, spread) in spreads.items():
        noise = np.random.default_rng([zlib.crc32(name.encode()), seed]).standard_normal(out[name].shape)
        drawn = base * np.exp(spread * noise) if base else spread * noise
        out[name] = jnp.asarray(drawn.astype(out[name].dtype))
    for name, factor in factors.items():
        out[name] = (out[name] * factor).astype(out[name].dtype)
    return out
```

```python
import concourse.bass as bass
from concourse import mybir
from contextlib import ExitStack


def build(nc, x, adj, nodemask, l0_wv, l0_bv, l0_aw, l0_ab, l0_wk, l0_bk, l1_w, l1_a,
          l2_w1, l2_b1, l2_w2, l2_b2, l2_w3, l2_b3, l3_wqkv, l3_wout, l3_bout, out):
    fp32 = mybir.dt.float32
    f32r = mybir.dt.float32r
    bf16 = mybir.dt.bfloat16
    ALU = mybir.AluOpType
    ACT = mybir.ActivationFunctionType
    AX = mybir.AxisListType

    GRAPHS, N, D = x.shape
    P = 128
    C = D // P
    G = 2
    PAIRS = GRAPHS // G
    HEADS = 8
    DH = l3_wout.shape[0] // HEADS
    INNER = HEADS * DH
    HP = HEADS // 2
    KHOPS = l0_wk.shape[0]
    EXT = D + 2
    EPS = 1e-5
    ROW_EPS = 1e-12
    SLOPE = 0.2
    NEG_INF = -9e15
    CAP = 3e38
    BIG = 2.0 ** 127
    SCALE = float(DH) ** -0.5
    LA = LG = 0.33

    ctx = ExitStack()
    with ctx:
        def sb(name, shape, dt=fp32):
            return ctx.enter_context(nc.sbuf_tensor(name, shape, dt))

        ident = sb("ident", [P, P])
        stage = sb("stage", [P, 3 * C * INNER])
        w_raw = stage[:, :].rearrange("p (c n) -> p c n", c=C)
        wv_raw = sb("wv_raw", [P, C, D])
        aw_bc = sb("aw_bc", [P, 2, D])
        a_bc = sb("a_bc", [P, 2, D])
        bv_bc = sb("bv_bc", [P, D])
        ab_bc = sb("ab_bc", [P, 1])
        bk_bc = sb("bk_bc", [P, KHOPS, D])
        stage2 = sb("stage2", [P, 10 * D])
        junk = stage2[:, :].rearrange("p (k n) -> p k n", k=10)
        att0 = sb("att0", [P, C, 2])
        att1 = sb("att1", [P, C, 2])
        c_part = sb("c_part", [P, 3])
        c0 = sb("c0", [P, 1])
        k_hi = sb("k_hi", [P, C, KHOPS, EXT], f32r)
        k_lo = sb("k_lo", [P, C, KHOPS, EXT], f32r)
        w1_hi = sb("w1_hi", [P, C, EXT], f32r)
        w1_lo = sb("w1_lo", [P, C, EXT], f32r)
        v0_hi = sb("v0_hi", [P, C, P], f32r)
        v0_lo = sb("v0_lo", [P, C, P], f32r)
        v1_hi = sb("v1_hi", [P, C, P], f32r)
        v1_lo = sb("v1_lo", [P, C, P], f32r)
        g1 = sb("g1", [P, C, D])
        g2 = sb("g2", [P, C, D])
        g3 = sb("g3", [P, C, D])
        gb1 = sb("gb1", [P, C])
        gb2 = sb("gb2", [P, C])
        b3_bc = sb("b3_bc", [P, D])
        qkv_hi = sb("qkv_hi", [P, C, 3 * INNER], f32r)
        qkv_lo = sb("qkv_lo", [P, C, 3 * INNER], f32r)
        wout = sb("wout", [P, HP, D])
        bout_bc = sb("bout_bc", [P, D])
        bsum = sb("bsum", [P, D])
        bsum_a = sb("bsum_a", [P, D])
        spare = sb("spare", [P, 1])
        zero = sb("zero", [P, 1])
        expo = sb("expo", [P, G])

        x0 = sb("x0", [P, G, D])
        adj_ij = sb("adj_ij", [P, G, N])
        mask_u8 = sb("mask_u8", [1, G * N], mybir.dt.uint8)
        stats = [sb(f"stats{k}", [P, G, 6]) for k in range(4)]
        mv = [sb(f"mv{k}", [P, G, 2]) for k in range(4)]
        veps = [sb(f"veps{k}", [P, G]) for k in range(4)]
        rstd = [sb(f"rstd{k}", [P, G]) for k in range(4)]
        hn = [sb(f"hn{k}", [P, G, D]) for k in range(4)]
        h2 = sb("h2", [P, G, D])
        h0_hi = sb("h0_hi", [P, C, G, N], f32r)
        h0_lo = sb("h0_lo", [P, C, G, N], f32r)
        h1_hi = sb("h1_hi", [P, C, G, N], f32r)
        h1_lo = sb("h1_lo", [P, C, G, N], f32r)
        h3_hi = sb("h3_hi", [P, C, G, N], f32r)
        h3_lo = sb("h3_lo", [P, C, G, N], f32r)
        adj_ji = sb("adj_ji", [P, G, N])
        adjs = sb("adjs", [P, G, N])
        sic = sb("sic", [P, G])
        z0 = sb("z0", [P, G, N])
        l0 = sb("l0", [P, G, N])
        e0 = sb("e0", [P, G, N])
        alpha = sb("alpha", [P, G, N])
        rsum = sb("rsum", [P, G])
        rsume = sb("rsume", [P, G])
        rinv = sb("rinv", [P, G])
        tr = sb("tr", [P, G, N])
        trT = sb("trT", [P, G, N])
        s2 = sb("s2", [P, G, D])
        s1 = sb("s1", [P, G, D])
        xt = sb("xt", [P, G, D])
        x1 = sb("x1", [P, G, D])
        cap = sb("cap", [P, G, N])
        wh2 = sb("wh2", [P, G])
        z1 = sb("z1", [P, G, N])
        l1 = sb("l1", [P, G, N])
        em = sb("em", [P, G, N])
        nmax1 = sb("nmax1", [P, G])
        p1 = sb("p1", [P, G, N])
        den1 = sb("den1", [P, G])
        rden1 = sb("rden1", [P, G])
        whs = sb("whs", [P, G, D])
        mn = sb("mn", [P, G, D])
        ex = sb("ex", [P, G, D])
        rx = sb("rx", [P, G, D])
        x2 = sb("x2", [P, G, D])
        x2b = sb("x2b", [P, G, D])
        zt = sb("zt", [P, C, G * N])
        y1 = sb("y1", [P, C, G * N])
        y2 = sb("y2", [P, C, G * N])
        sup = sb("sup", [P, G, D])
        x3 = sb("x3", [P, G, D])
        x3b = sb("x3b", [P, G, D])
        mrow = sb("mrow", [P, G, N], bf16)
        mrow0 = sb("mrow0", [P, G, N], bf16)
        mbig = sb("mbig", [P, G, N], bf16)
        ed = sb("ed", [P, G, N])
        bd = sb("bd", [P, G, N])
        bT = sb("bT", [P, G, N])
        qT = sb("qT", [P, HP, G, N])
        kbd = sb("kbd", [P, HP, G, 2, N])
        v = sb("v", [P, G, INNER])
        nm = sb("nm", [P, G, HEADS])
        nms = sb("nms", [P, G, HEADS])
        rs = sb("rs", [P, G, HEADS])
        ri = sb("ri", [P, G, HEADS])
        ri33 = sb("ri33", [P, G, HEADS])
        pr = stage[:, 0:G * HEADS * N].rearrange("p (g h n) -> p g h n", g=G, h=HEADS)
        pn = sb("pn", [P, G, HEADS, N])
        at = stage2[:, 0:G * HEADS * N].rearrange("p (g h n) -> p g h n", g=G, h=HEADS)
        ot = sb("ot", [P, G, HP, N])
        x4 = sb("x4", [P, G, D])

        f = ctx.enter_context(nc.psum_tensor("f", [P, 4, 512], fp32))
        s = ctx.enter_context(nc.psum_tensor("s", [P, 4, 512], fp32))

        BANKS = (2, 0)

        names = """w_in w_in2 w_in3 wv_used w_junk w_att w_c w_c0 w_bsa w_split w_ready pad_set pad2_set id_zero id_set
            mask_pad expo_set
            x_in adj_in mask_in out_done
            T_f1 adjT h0_hi h0_lo E0 S2p si z0 l0 e0 alpha rsume rinv tr TT trT U1 s2 A0 s1 U0 B0 xt x1
            T_h1 h1_hi h1_lo E1 Wh cap wh2 z1 l1 em nmax1 p1 rden1 whs Hp mn ex rx x2 h2 adjs x2b
            ZT MM zt Y1 y1 SA supa Y2 y2 SB supb OUT x3 x3b ed bd bT T_h3 h3_hi h3_lo
            Q q K k_even k_odd V v mrow dots0 dots1 nm0 nm1 nms0 nms1 pr0 pr1 ri0 ri1 ri33_0 ri33_1 pn0 pn1
            PT0 PT1 at0 at1 PV0 PV1 ot0 ot1 W x4""".split()
        sem = {n: ctx.enter_context(nc.semaphore(n)) for n in names}
        for k in range(4):
            for n in ("stats", "mv", "veps", "rstd", "hn"):
                sem[f"{n}{k}"] = ctx.enter_context(nc.semaphore(f"{n}_{k}"))

        block = ctx.enter_context(nc.Block())

        def pair_rows(a, t):
            if isinstance(t, int):
                return a[t * G:(t + 1) * G].rearrange("g n d -> n g d")
            return a[bass.ds(t * G, G)].rearrange("g n d -> n g d")

        def pair_mask(start):
            m = nodemask.rearrange("(a g) n -> a (g n)", a=1)
            return m[:, start:start + G * N] if isinstance(start, int) else m[:, bass.ds(start, G * N)]

        def per_graph(b):
            return b[:, :].unsqueeze(1).broadcast_to([P, G, D])

        LOADS1 = 11 + 2 * KHOPS
        LOADS2 = 3 * C

        @block.sync
        def _(sp):
            def row_bc(a, width):
                return a.rearrange("(a n) -> a n", a=1).broadcast_to([P, width])

            def load(t):
                sp.dma_start(x0[:, :, :], pair_rows(x, t)).then_inc(sem["x_in"], 16)
                sp.dma_start(adj_ij[:, :, :], pair_rows(adj, t)).then_inc(sem["adj_in"], 16)

            def load_mask(start):
                sp.dma_start(mask_u8[:, :], pair_mask(start)).then_inc(sem["mask_in"], 16)

            load(0)
            load_mask(0)
            n1 = [sp.dma_start(wv_raw[:, :, :], l0_wv.rearrange("(c p) n -> p c n", c=C)),
                  sp.dma_start(w_raw[:, :, 3 * D:4 * D], l1_w.rearrange("(c p) n -> p c n", c=C)),
                  sp.dma_start(bv_bc[:, :], row_bc(l0_bv, D)),
                  sp.dma_start(ab_bc[:, :], row_bc(l0_ab, 1))]
            for j in range(2):
                n1.append(sp.dma_start(aw_bc[:, j, :], row_bc(l0_aw[j * D:(j + 1) * D, :].rearrange("n a -> (n a)"), D)))
                n1.append(sp.dma_start(a_bc[:, j, :], row_bc(l1_a[j * D:(j + 1) * D, :].rearrange("n a -> (n a)"), D)))
            for k in range(KHOPS):
                n1.append(sp.dma_start(w_raw[:, :, k * D:(k + 1) * D], l0_wk[k].rearrange("(c p) n -> p c n", c=C)))
                n1.append(sp.dma_start(bk_bc[:, k, :], row_bc(l0_bk[k], D)))
            for d in n1:
                d.then_inc(sem["w_in"], 16)
            assert len(n1) == LOADS1 - 3
            n3 = [sp.dma_start(g[:, :, :], w.rearrange("(c p) n -> p c n", c=C))
                  for g, w in ((g1, l2_w1), (g2, l2_w2), (g3, l2_w3))]
            n3 += [sp.dma_start(g[:, :], b.rearrange("(c p) -> p c", c=C), allow_slow_non_contiguous=True) for g, b in ((gb1, l2_b1), (gb2, l2_b2))]
            n3 += [sp.dma_start(b3_bc[:, :], row_bc(l2_b3, D)), sp.dma_start(bout_bc[:, :], row_bc(l3_bout, D)),
                   sp.dma_start(wout[:, :, :], l3_wout.rearrange("(c p) n -> p c n", c=HP))]
            for d in n3:
                d.then_inc(sem["w_in3"], 16)
            sp.wait_ge(sem["w_split"], 1)
            for c in range(C):
                for kind in range(3):
                    src = l3_wqkv[c * P:(c + 1) * P, :].rearrange("p (h k d) -> p h k d", h=HEADS, k=3)[:, :, kind, :]
                    dst = w_raw[:, c, kind * INNER:(kind + 1) * INNER].rearrange("p (h d) -> p h d", h=HEADS)
                    sp.dma_start(dst, src).then_inc(sem["w_in2"], 16)

            def next_pair(t, n):
                sp.wait_ge(sem["x1"], n)
                load(t)
                sp.wait_ge(sem["mrow"], n)
                load_mask(t * G * N)

            def store(t, n):
                sp.wait_ge(sem["x4"], n + 1)
                sp.dma_start(pair_rows(out, t), x4[:, :, :]).then_inc(sem["out_done"], 16)

            next_pair(1, 1)
            sp.sem_inc(sem["out_done"], 16)
            sp.sem_inc(sem["x4"], 1)
            with sp.Fori(1, PAIRS - 1) as t:
                sp.wait_ge(sem["x1"], t + 1)
                load(t + 1)
                store(t - 1, t)
                sp.wait_ge(sem["mrow"], t + 1)
                load_mask(t * (G * N) + G * N)
            store(PAIRS - 2, PAIRS - 1)
            store(PAIRS - 1, PAIRS)
            sp.wait_ge(sem["out_done"], 16 * (PAIRS + 1))

        @block.gpsimd
        def _(gp):
            gp.memset(zero[:, :], 0.0)
            gp.memset(expo[:, :], -0.5).then_inc(sem["expo_set"], 1)
            gp.memset(ident[:, :], 0.0).then_inc(sem["id_zero"], 1)
            gp.wait_ge(sem["id_zero"], 1)
            gp.affine_select(out=ident[:, :], in_=ident[:, :], compare_op=ALU.not_equal, fill=1.0,
                             base=0, pattern=[[-1, P]], channel_multiplier=1).then_inc(sem["id_set"], 1)
            gp.memset(kbd[:, :, :, :, :], 0.0).then_inc(sem["pad_set"], 1)
            gp.wait_ge(sem["expo_set"], 1)
            gp.wait_ge(sem["w_in3"], 16 * 8)

            def power(k, n):
                gp.wait_ge(sem[f"veps{k}"], n)
                gp.tensor_tensor(rstd[k][:, :], veps[k][:, :], expo[:, :], ALU.pow).then_inc(sem[f"rstd{k}"], 1)

            def distance(n):
                gp.wait_ge(sem["ed"], n)
                gp.tensor_tensor(bd[:, :, :], adjs[:, :, :], ed[:, :, :], ALU.add).then_inc(sem["bd"], 1)

            def x3_bias(n):
                gp.wait_ge(sem["x3"], n)
                gp.tensor_tensor(x3b[:, :, :], x3[:, :, :], per_graph(bout_bc), ALU.add).then_inc(sem["x3b"], 1)

            def probs(g, n):
                gp.wait_ge(sem[f"ri33_{g}"], n)
                gp.tensor_tensor(pn[:, g, :, :], pr[:, g, :, :],
                                 ri33[:, g, :].unsqueeze(2).broadcast_to([P, HEADS, N]), ALU.mult).then_inc(sem[f"pn{g}"], 1)

            def hand_over(n, prev):
                if prev is not None:
                    gp.wait_ge(sem["bT"], prev)
                    gp.wait_ge(sem["OUT"], prev)
                    gp.wait_ge(sem["x3"], prev)
                gp.wait_ge(sem["adjT"], n)
                gp.tensor_tensor(adjs[:, :, :], adj_ji[:, :, :], zero[:, :].unsqueeze(2).broadcast_to([P, G, N]), ALU.add).then_inc(sem["adjs"], 1)
                gp.wait_ge(sem["x2"], n)
                gp.tensor_tensor(x2b[:, :, :], x2[:, :, :], per_graph(b3_bc), ALU.add).then_inc(sem["x2b"], 1)

            power(0, 1)
            power(1, 1)
            hand_over(1, None)
            power(2, 1)
            with gp.Fori(1, PAIRS) as t:
                power(0, t + 1)
                distance(t)
                power(3, t)
                x3_bias(t)
                power(1, t + 1)
                probs(0, t)
                probs(1, t)
                power(2, t + 1)
                hand_over(t + 1, t)
            distance(PAIRS)
            power(3, PAIRS)
            x3_bias(PAIRS)
            probs(0, PAIRS)
            probs(1, PAIRS)

        @block.scalar
        def _(act):
            def copy(o, i):
                return act.activation(o, i, ACT.Copy)

            def f_transposed(n, prev):
                act.wait_ge(sem["T_f1"], n)
                if prev is not None:
                    act.wait_ge(sem["cap"], prev)
                    act.wait_ge(sem["adjs"], prev)
                copy(adj_ji[:, :, :], f[:, 1, 0:G * N]).then_inc(sem["adjT"], 1)
                act.activation(h0_hi[:, :, :, :], f[:, 0, :], ACT.Relu).then_inc(sem["h0_hi"], 1)

            def f_s2(n):
                act.wait_ge(sem["si"], n)
                copy(s2[:, :, :], f[:, 2:4, 0:D]).then_inc(sem["s2"], 1)

            def f_exp0(n):
                act.wait_ge(sem["l0"], n)
                act.activation(e0[:, :, :], l0[:, :, :], ACT.Exp).then_inc(sem["e0"], 1)

            def f_trT(n):
                act.wait_ge(sem["TT"], n)
                copy(trT[:, :, :], f[:, 1, 0:G * N]).then_inc(sem["trT"], 1)

            def f_s1(n):
                act.wait_ge(sem["A0"], n)
                copy(s1[:, :, :], f[:, 0, :]).then_inc(sem["s1"], 1)

            def f_h1(n):
                act.wait_ge(sem["T_h1"], n)
                act.activation(h1_hi[:, :, :, :], f[:, 0, :], ACT.Relu).then_inc(sem["h1_hi"], 1)

            def f_att1(n):
                act.wait_ge(sem["nmax1"], n)
                for g in range(G):
                    p = act.activation(p1[:, g, :], em[:, g, :], ACT.Exp, bias=nmax1[:, g:g + 1],
                                       accum_out=den1[:, g:g + 1])
                p.then_inc(sem["p1"], 1)
                act.wait_ge(sem["rden1"], n)
                for g in range(G):
                    w = act.activation(whs[:, g, :], f[:, 2 + g, 0:D], ACT.Copy, scale=rden1[:, g:g + 1])
                w.then_inc(sem["whs"], 1)

            def f_elu(n):
                act.wait_ge(sem["mn"], n)
                act.activation(ex[:, :, :], mn[:, :, :], ACT.Exp).then_inc(sem["ex"], 1)

            def s_zt(n):
                act.wait_ge(sem["ZT"], n)
                copy(zt[:, :, :], s[:, 0, :]).then_inc(sem["zt"], 1)
                act.activation(ed[:, :, :], adjs[:, :, :], ACT.Exp, scale=-1.0).then_inc(sem["ed"], 1)

            def s_relu(made, bank, bias, y, done, n):
                act.wait_ge(sem[made], n)
                for c in range(C):
                    r = act.activation(y[:, c, :], s[:, bank, c * G * N:(c + 1) * G * N], ACT.Relu, bias=bias[:, c:c + 1])
                r.then_inc(sem[done], 1)

            def s_sup(made, bank, done, n):
                act.wait_ge(sem[made], n)
                copy(sup[:, :, :], s[:, bank, :]).then_inc(sem[done], 1)

            def s_h3(n):
                act.wait_ge(sem["T_h3"], n)
                act.activation(h3_hi[:, :, :, :], s[:, 2, :], ACT.Relu).then_inc(sem["h3_hi"], 1)

            def s_q(n):
                act.wait_ge(sem["Q"], n)
                copy(qT[:, :, :, :], s[:, 0:2, :]).then_inc(sem["q"], 1)

            def s_k_even(n):
                act.wait_ge(sem["K"], n)
                copy(kbd[0:DH, :, :, 0, :], s[0:DH, 2:4, :].rearrange("p b (q n) -> p (b q) n", n=N))\
                    .then_inc(sem["k_even"], 1)

            def s_v(n):
                act.wait_ge(sem["V"], n)
                copy(v[:, :, :], s[:, 0:2, :]).then_inc(sem["v"], 1)

            def s_exps(g, n):
                act.wait_ge(sem[f"nms{g}"], n)
                for h in range(HEADS):
                    e = act.activation(pr[:, g, h, :], s[:, BANKS[g] + h // 4, (h % 4) * N:(h % 4 + 1) * N], ACT.Exp,
                                       bias=nms[:, g, h:h + 1], scale=SCALE, accum_out=rs[:, g, h:h + 1])
                e.then_inc(sem[f"pr{g}"], 1)

            def s_ot(g, n):
                act.wait_ge(sem[f"PV{g}"], n)
                copy(ot[:, g, :, :], s[:, BANKS[g], :]).then_inc(sem[f"ot{g}"], 1)

            act.wait_ge(sem["w_in3"], 16 * 8)
            f_transposed(1, None)
            f_s2(1)
            f_exp0(1)
            f_trT(1)
            f_s1(1)
            f_h1(1)
            f_att1(1)
            f_elu(1)
            with act.Fori(1, PAIRS) as t:
                s_zt(t)
                s_relu("Y1", 1, gb1, y1, "y1", t)
                f_transposed(t + 1, t)
                s_sup("SA", 2, "supa", t)
                f_s2(t + 1)
                s_relu("Y2", 3, gb2, y2, "y2", t)
                f_exp0(t + 1)
                s_sup("SB", 0, "supb", t)
                f_trT(t + 1)
                f_s1(t + 1)
                s_h3(t)
                s_q(t)
                f_h1(t + 1)
                s_k_even(t)
                s_v(t)
                s_exps(0, t)
                f_att1(t + 1)
                s_exps(1, t)
                f_elu(t + 1)
                s_ot(0, t)
                s_ot(1, t)
            n = PAIRS
            s_zt(n)
            s_relu("Y1", 1, gb1, y1, "y1", n)
            s_sup("SA", 2, "supa", n)
            s_relu("Y2", 3, gb2, y2, "y2", n)
            s_sup("SB", 0, "supb", n)
            s_h3(n)
            s_q(n)
            s_k_even(n)
            s_v(n)
            s_exps(0, n)
            s_exps(1, n)
            s_ot(0, n)
            s_ot(1, n)

        @block.vector
        def _(dve):
            dve.wait_ge(sem["w_in"], 16 * (LOADS1 - 3))
            wl1 = w_raw[:, :, 3 * D:4 * D]
            k = 0
            for c in range(C):
                for j in range(2):
                    dve.tensor_tensor_reduce(out=junk[:, k, :], in0=wv_raw[:, c, :], in1=aw_bc[:, j, :], scale=1.0,
                                             scalar=0.0, op0=ALU.mult, op1=ALU.add, accum_out=att0[:, c, j:j + 1])
                    dve.tensor_tensor_reduce(out=junk[:, k + 1, :], in0=wl1[:, c, :], in1=a_bc[:, j, :], scale=1.0,
                                             scalar=0.0, op0=ALU.mult, op1=ALU.add, accum_out=att1[:, c, j:j + 1])
                    k += 2
            for j in range(2):
                last = dve.tensor_tensor_reduce(out=junk[:, k + j, :], in0=bv_bc[:, :], in1=aw_bc[:, j, :], scale=1.0,
                                                scalar=0.0, op0=ALU.mult, op1=ALU.add, accum_out=c_part[:, j:j + 1])
            last.then_inc(sem["w_att"], 1)
            dve.wait_ge(sem["w_att"], 1)
            dve.tensor_tensor(c_part[:, 2:3], c_part[:, 0:1], c_part[:, 1:2], ALU.add).then_inc(sem["w_c"], 1)
            dve.tensor_tensor(bsum_a[:, :], bk_bc[:, 0, :], bk_bc[:, 1, :], ALU.add).then_inc(sem["w_bsa"], 1)
            dve.wait_ge(sem["w_c"], 1)
            dve.tensor_tensor(c0[:, :], c_part[:, 2:3], ab_bc[:, :], ALU.add).then_inc(sem["w_c0"], 1)
            dve.wait_ge(sem["w_bsa"], 1)
            dve.tensor_tensor(bsum[:, :], bsum_a[:, :], bk_bc[:, 2, :], ALU.add)
            zero_col = [(k_hi, k_lo), (w1_hi, w1_lo)]
            for hi, lo in zero_col:
                for w in (hi, lo):
                    tail = w[:, :, :, D + 1:EXT] if w in (k_hi, k_lo) else w[:, :, D + 1:EXT]
                    last = dve.memset(tail.bitcast(fp32), 0.0)
            last.then_inc(sem["pad2_set"], 1)

            def hi_part(hi, full):
                return dve.tensor_copy(hi, full)

            def lo_part(lo, full, hi):
                return dve.tensor_tensor(lo, full, hi.bitcast(fp32), ALU.subtract)

            cols0 = [(k_hi[:, :, j, 0:D], k_lo[:, :, j, 0:D], w_raw[:, :, j * D:(j + 1) * D]) for j in range(KHOPS)]
            cols1 = [(k_hi[:, :, j, D:D + 1], k_lo[:, :, j, D:D + 1], att0[:, :, 1:2]) for j in range(KHOPS)]
            cols2 = [(w1_hi[:, :, 0:D], w1_lo[:, :, 0:D], wl1), (w1_hi[:, :, D:D + 1], w1_lo[:, :, D:D + 1], att1[:, :, 1:2])]
            cols3 = [(v0_hi[:, :, :], v0_lo[:, :, :], att0[:, :, 0:1].broadcast_to([P, C, P])),
                     (v1_hi[:, :, :], v1_lo[:, :, :], att1[:, :, 0:1].broadcast_to([P, C, P]))]
            parts = cols0 + cols1 + cols2 + cols3
            for hi, lo, full in parts:
                last = hi_part(hi, full)
            last.then_inc(sem["w_junk"], 1)
            dve.wait_ge(sem["w_junk"], 1)
            for hi, lo, full in parts:
                last = lo_part(lo, full, hi)
            last.then_inc(sem["w_split"], 1)
            dve.memset(mrow0[:, :, :], 0.0)
            dve.memset(mrow[:, :, :], 0.0)
            dve.memset(mbig[:, :, :], 0.0).then_inc(sem["mask_pad"], 1)
            dve.wait_ge(sem["mask_pad"], 1)
            dve.memset(mrow[0:2, :, :], 1.0)
            dve.memset(mbig[0:2, :, :], -BIG).then_inc(sem["mask_pad"], 1)
            dve.wait_ge(sem["w_in2"], 16 * LOADS2)
            hi_part(qkv_hi[:, :, :], w_raw[:, :, :]).then_inc(sem["w_junk"], 1)
            dve.wait_ge(sem["w_junk"], 2)
            lo_part(qkv_lo[:, :, :], w_raw[:, :, :], qkv_hi[:, :, :]).then_inc(sem["w_ready"], 1)
            dve.wait_ge(sem["mask_pad"], 2)

            def norm_stats(k, src, n):
                for g in range(G):
                    b = dve.bn_stats(stats[k][:, g, :], src[:, g, :])
                b.then_inc(sem[f"stats{k}"], 1)
                dve.wait_ge(sem[f"stats{k}"], n)
                dve.memset(spare[:, :], 0.0)
                for g in range(G):
                    b = dve.bn_aggr(mv[k][:, g, :], stats[k][:, g, :])
                b.then_inc(sem[f"mv{k}"], 1)
                dve.wait_ge(sem[f"mv{k}"], n)
                dve.tensor_scalar(veps[k][:, :], mv[k][:, :, 1], EPS, None, ALU.add).then_inc(sem[f"veps{k}"], 1)

            def norm_apply(k, src, n):
                dve.wait_ge(sem[f"rstd{k}"], n)
                for g in range(G):
                    b = dve.tensor_scalar(hn[k][:, g, :], src[:, g, :], mv[k][:, g, 0:1], rstd[k][:, g:g + 1],
                                          ALU.subtract, ALU.mult)
                b.then_inc(sem[f"hn{k}"], 1)

            def lo_relu(k, bank, hi, lo, n):
                dve.wait_ge(sem[f"h{k}_hi"], n)
                dve.scalar_tensor_tensor(lo[:, :, :, :].rearrange("p c g n -> p (c g n)"), bank, 0.0,
                                         hi[:, :, :, :].bitcast(fp32).rearrange("p c g n -> p (c g n)"),
                                         ALU.max, ALU.subtract).then_inc(sem[f"h{k}_lo"], 1)

            def f_norm0(n):
                dve.wait_ge(sem["x_in"], 16 * n)
                norm_stats(0, x0, n)

            def f_logits0(n):
                dve.wait_ge(sem["S2p"], n)
                dve.tensor_scalar(sic[:, :], f[:, 2:4, D], c0[:, 0:1], None, ALU.add).then_inc(sem["si"], 1)
                dve.wait_ge(sem["si"], n)
                for g in range(G):
                    z = dve.tensor_scalar(z0[:, g, :], f[:, 1, g * N:(g + 1) * N], sic[:, g:g + 1], None, ALU.add)
                z.then_inc(sem["z0"], 1)
                dve.wait_ge(sem["z0"], n)
                dve.scalar_tensor_tensor(l0[:, :, :], z0[:, :, :], SLOPE, z0[:, :, :], ALU.mult, ALU.max)\
                    .then_inc(sem["l0"], 1)

            def f_transition(n):
                dve.wait_ge(sem["e0"], n)
                dve.wait_ge(sem["adj_in"], 16 * n)
                for g in range(G):
                    a = dve.tensor_tensor_reduce(out=alpha[:, g, :], in0=e0[:, g, :], in1=adj_ij[:, g, :], scale=1.0,
                                                 scalar=0.0, op0=ALU.mult, op1=ALU.add, accum_out=rsum[:, g:g + 1])
                a.then_inc(sem["alpha"], 1)
                dve.wait_ge(sem["alpha"], n)
                dve.tensor_scalar(rsume[:, :], rsum[:, :], ROW_EPS, None, ALU.add).then_inc(sem["rsume"], 1)
                dve.wait_ge(sem["rsume"], n)
                dve.reciprocal(rinv[:, :], rsume[:, :]).then_inc(sem["rinv"], 1)
                dve.wait_ge(sem["rinv"], n)
                for g in range(G):
                    a = dve.tensor_scalar(tr[:, g, :], alpha[:, g, :], rinv[:, g:g + 1], None, ALU.mult)
                a.then_inc(sem["tr"], 1)

            def f_x1(n):
                dve.wait_ge(sem["B0"], n)
                dve.tensor_tensor(xt[:, :, :], f[:, 2, :].rearrange("p (g d) -> p g d", g=G), per_graph(bsum), ALU.add)\
                    .then_inc(sem["xt"], 1)
                dve.wait_ge(sem["xt"], n)
                dve.scalar_tensor_tensor(x1[:, :, :], xt[:, :, :], 0.0, x0[:, :, :], ALU.max, ALU.add)\
                    .then_inc(sem["x1"], 1)

            def f_cap(n):
                dve.wait_ge(sem["adjT"], n)
                dve.tensor_scalar(cap[:, :, :], adj_ji[:, :, :], 0.5, CAP, ALU.is_gt, ALU.mult).then_inc(sem["cap"], 1)

            def f_logits1(n):
                dve.wait_ge(sem["Wh"], n)
                dve.tensor_copy(wh2[:, :], f[:, 2:4, D]).then_inc(sem["wh2"], 1)
                dve.wait_ge(sem["wh2"], n)
                for g in range(G):
                    z = dve.tensor_scalar(z1[:, g, :], f[:, 1, g * N:(g + 1) * N], wh2[:, g:g + 1], None, ALU.add)
                z.then_inc(sem["z1"], 1)
                dve.wait_ge(sem["z1"], n)
                dve.scalar_tensor_tensor(l1[:, :, :], z1[:, :, :], SLOPE, z1[:, :, :], ALU.mult, ALU.max)\
                    .then_inc(sem["l1"], 1)
                dve.wait_ge(sem["l1"], n)
                dve.wait_ge(sem["cap"], n)
                dve.scalar_tensor_tensor(em[:, :, :], cap[:, :, :], NEG_INF, l1[:, :, :], ALU.add, ALU.min)\
                    .then_inc(sem["em"], 1)
                dve.wait_ge(sem["em"], n)
                dve.tensor_reduce(nmax1[:, :], em[:, :, :], AX.X, ALU.max, negate=True).then_inc(sem["nmax1"], 1)

            def f_rden(n):
                dve.wait_ge(sem["p1"], n)
                dve.reciprocal(rden1[:, :], den1[:, :]).then_inc(sem["rden1"], 1)

            def f_x2(n):
                dve.wait_ge(sem["Hp"], n)
                dve.tensor_scalar(mn[:, :, :], f[:, 0, :].rearrange("p (g d) -> p g d", g=G), 0.0, None, ALU.min)\
                    .then_inc(sem["mn"], 1)
                dve.scalar_tensor_tensor(rx[:, :, :], f[:, 0, :].rearrange("p (g d) -> p g d", g=G), 0.0, x1[:, :, :],
                                         ALU.max, ALU.add).then_inc(sem["rx"], 1)
                dve.wait_ge(sem["rx"], n)
                dve.wait_ge(sem["ex"], n)
                dve.scalar_tensor_tensor(x2[:, :, :], ex[:, :, :], -1.0, rx[:, :, :], ALU.add, ALU.add)\
                    .then_inc(sem["x2"], 1)

            def f_h2(n):
                norm_apply(2, x2, n)
                dve.wait_ge(sem["hn2"], n)
                dve.tensor_scalar(h2[:, :, :], hn[2][:, :, :], 0.0, None, ALU.max).then_inc(sem["h2"], 1)

            def f_mask(n):
                dve.wait_ge(sem["mask_in"], 16 * n)
                m = mask_u8[:, :].rearrange("a (g n) -> a g n", g=G)
                dve.tensor_copy(mrow[0:1, :, :], m)
                dve.tensor_copy(mrow0[0:1, :, :], m)
                dve.tensor_scalar(mbig[0:1, :, :], m, BIG, None, ALU.mult).then_inc(sem["mrow"], 1)

            def s_bT(n):
                dve.wait_ge(sem["MM"], n)
                dve.wait_ge(sem["bd"], n)
                dve.scalar_tensor_tensor(bT[:, :, :], bd[:, :, :], LG, s[:, 3, 0:G * N].rearrange("p (g n) -> p g n", g=G),
                                         ALU.mult, ALU.mult).then_inc(sem["bT"], 1)

            def s_x3(n):
                dve.wait_ge(sem["OUT"], n)
                dve.wait_ge(sem["x2b"], n)
                dve.tensor_tensor(x3[:, :, :], s[:, 1, :].rearrange("p (g d) -> p g d", g=G), x2b[:, :, :], ALU.add)\
                    .then_inc(sem["x3"], 1)
                dve.wait_ge(sem["x3"], n)

            def s_k_odd(n):
                dve.wait_ge(sem["K"], n)
                dve.tensor_copy(kbd[DH:P, :, :, 1, :], s[DH:P, 2:4, :].rearrange("p b (q n) -> p (b q) n", n=N))\
                    .then_inc(sem["k_odd"], 1)

            def s_max(g, n):
                dve.wait_ge(sem[f"dots{g}"], n)
                dve.tensor_reduce(nm[:, g, :], s[:, BANKS[g]:BANKS[g] + 2, :].rearrange("p b (h n) -> p (b h) n", n=N),
                                  AX.X, ALU.max).then_inc(sem[f"nm{g}"], 1)
                dve.wait_ge(sem[f"nm{g}"], n)
                dve.tensor_scalar(nms[:, g, :], nm[:, g, :], -SCALE, None, ALU.mult).then_inc(sem[f"nms{g}"], 1)

            def s_rsum(g, n):
                dve.wait_ge(sem[f"pr{g}"], n)
                dve.reciprocal(ri[:, g, :], rs[:, g, :]).then_inc(sem[f"ri{g}"], 1)
                dve.wait_ge(sem[f"ri{g}"], n)
                dve.tensor_scalar(ri33[:, g, :], ri[:, g, :], LA, None, ALU.mult).then_inc(sem[f"ri33_{g}"], 1)

            def s_at(g, n):
                dve.wait_ge(sem[f"PT{g}"], n)
                dve.tensor_tensor(at[:, g, :, :], s[:, BANKS[g]:BANKS[g] + 2, :].rearrange("p b (h n) -> p (b h) n", n=N),
                                  bT[:, g, :].unsqueeze(1).broadcast_to([P, HEADS, N]), ALU.add).then_inc(sem[f"at{g}"], 1)

            def s_x4(n, stored):
                dve.wait_ge(sem["W"], n)
                dve.wait_ge(sem["x3b"], n)
                dve.wait_ge(sem["out_done"], stored)
                dve.tensor_tensor(x4[:, :, :], s[:, 3, :].rearrange("p (g d) -> p g d", g=G), x3b[:, :, :], ALU.add)\
                    .then_inc(sem["x4"], 1)

            f_norm0(1)
            norm_apply(0, x0, 1)
            lo_relu(0, f[:, 0, :], h0_hi, h0_lo, 1)
            f_logits0(1)
            f_transition(1)
            f_cap(1)
            f_x1(1)
            dve.wait_ge(sem["x1"], 1)
            norm_stats(1, x1, 1)
            norm_apply(1, x1, 1)
            lo_relu(1, f[:, 0, :], h1_hi, h1_lo, 1)
            f_logits1(1)
            f_rden(1)
            f_x2(1)
            dve.wait_ge(sem["x2"], 1)
            norm_stats(2, x2, 1)
            f_h2(1)
            f_mask(1)
            dve.wait_ge(sem["mrow"], 1)
            with dve.Fori(1, PAIRS) as t:
                f_norm0(t + 1)
                norm_apply(0, x0, t + 1)
                s_bT(t)
                lo_relu(0, f[:, 0, :], h0_hi, h0_lo, t + 1)
                f_cap(t + 1)
                f_logits0(t + 1)
                f_transition(t + 1)
                s_x3(t)
                norm_stats(3, x3, t)
                norm_apply(3, x3, t)
                f_x1(t + 1)
                lo_relu(3, s[:, 2, :], h3_hi, h3_lo, t)
                dve.wait_ge(sem["x1"], t + 1)
                norm_stats(1, x1, t + 1)
                norm_apply(1, x1, t + 1)
                s_k_odd(t)
                lo_relu(1, f[:, 0, :], h1_hi, h1_lo, t + 1)
                s_max(0, t)
                f_logits1(t + 1)
                s_max(1, t)
                s_rsum(0, t)
                f_rden(t + 1)
                f_x2(t + 1)
                s_rsum(1, t)
                dve.wait_ge(sem["x2"], t + 1)
                norm_stats(2, x2, t + 1)
                s_at(0, t)
                f_h2(t + 1)
                f_mask(t + 1)
                s_at(1, t)
                s_x4(t, 16 * t)
            n = PAIRS
            s_bT(n)
            s_x3(n)
            norm_stats(3, x3, n)
            norm_apply(3, x3, n)
            lo_relu(3, s[:, 2, :], h3_hi, h3_lo, n)
            s_k_odd(n)
            s_max(0, n)
            s_max(1, n)
            s_rsum(0, n)
            s_rsum(1, n)
            s_at(0, n)
            s_at(1, n)
            s_x4(n, 16 * n)

        @block.tensor
        def _(pe):
            def mm(o, lhsT, rhs, start=True, stop=True, **kw):
                return pe.matmul(o, lhsT, rhs, start=start, stop=stop, **kw)

            def chunks3(o, pairs, start=True, stop=True, **kw):
                for i, (lh, ll, rh, rl) in enumerate(pairs):
                    mm(o, ll, rh, start=start and i == 0, stop=False, **kw)
                    mm(o, lh, rl, start=False, stop=False, **kw)
                    last = mm(o, lh, rh, start=False, stop=stop and i == len(pairs) - 1, **kw)
                return last

            def transposes(bank, tile):
                for c in range(C):
                    for g in range(G):
                        o = (c * G + g) * N
                        last = pe.transpose(bank[:, o:o + N], tile[:, g, c * P:(c + 1) * P], ident[:, :])
                return last

            def by_node(hi, lo, g, w_hi, w_lo):
                return [(hi[:, c, g, :], lo[:, c, g, :], w_hi(c), w_lo(c)) for c in range(C)]

            def f_transpose(n, prev):
                pe.wait_ge(sem["adj_in"], 16 * n)
                if prev is not None:
                    pe.wait_ge(sem["x2"], prev)
                for g in range(G):
                    pe.transpose(f[:, 1, g * N:(g + 1) * N], adj_ij[:, g, :], ident[:, :])
                pe.wait_ge(sem["hn0"], n)
                transposes(f[:, 0, :], hn[0]).then_inc(sem["T_f1"], 1)

            def f_products0(n):
                pe.wait_ge(sem["h0_lo"], n)
                chunks3(f[:, 1, 0:G * N], [(v0_hi[:, c, :], v0_lo[:, c, :], h0_hi[:, c, :, :], h0_lo[:, c, :, :])
                                           for c in range(C)])
                for g in range(G):
                    last = chunks3(f[:, 2 + g, 0:EXT], by_node(h0_hi, h0_lo, g, lambda c: k_hi[:, c, 2, :],
                                                               lambda c: k_lo[:, c, 2, :]))
                last.then_inc(sem["S2p"], 1)

            def f_hop1(n):
                for g in range(G):
                    chunks3(f[:, 0, g * D:(g + 1) * D], by_node(h0_hi, h0_lo, g, lambda c: k_hi[:, c, 1, 0:D],
                                                                lambda c: k_lo[:, c, 1, 0:D]),
                            start=(g == 0), stop=False, skip_group_check=True)

            def f_trT(n):
                pe.wait_ge(sem["tr"], n)
                for g in range(G):
                    last = pe.transpose(f[:, 1, g * N:(g + 1) * N], tr[:, g, :], ident[:, :])
                last.then_inc(sem["TT"], 1)

            def f_aggregate(bank, src, made, done, n):
                pe.wait_ge(sem["trT"], n)
                pe.wait_ge(sem[made], n)
                for g in range(G):
                    last = mm(f[:, bank, g * D:(g + 1) * D], trT[:, g, :], src[:, g, :], start=False,
                              skip_group_check=True)
                last.then_inc(sem[done], 1)

            def f_hop0(n):
                pe.wait_ge(sem["s2"], n)
                for g in range(G):
                    chunks3(f[:, 2, g * D:(g + 1) * D], by_node(h0_hi, h0_lo, g, lambda c: k_hi[:, c, 0, 0:D],
                                                                lambda c: k_lo[:, c, 0, 0:D]),
                            start=(g == 0), stop=False, skip_group_check=True)

            def f_transpose1(n):
                pe.wait_ge(sem["hn1"], n)
                transposes(f[:, 0, :], hn[1]).then_inc(sem["T_h1"], 1)

            def f_products1(n):
                pe.wait_ge(sem["h1_lo"], n)
                chunks3(f[:, 1, 0:G * N], [(v1_hi[:, c, :], v1_lo[:, c, :], h1_hi[:, c, :, :], h1_lo[:, c, :, :])
                                           for c in range(C)])
                for g in range(G):
                    last = chunks3(f[:, 2 + g, 0:EXT], by_node(h1_hi, h1_lo, g, lambda c: w1_hi[:, c, :],
                                                               lambda c: w1_lo[:, c, :]))
                last.then_inc(sem["Wh"], 1)

            def f_attend1(n):
                pe.wait_ge(sem["whs"], n)
                for g in range(G):
                    last = mm(f[:, 0, g * D:(g + 1) * D], p1[:, g, :], whs[:, g, :])
                last.then_inc(sem["Hp"], 1)

            def s_aggregate_h(n):
                pe.wait_ge(sem["h2"], n)
                pe.wait_ge(sem["adjs"], n)
                for c in range(C):
                    for g in range(G):
                        o = (c * G + g) * N
                        last = mm(s[:, 0, o:o + N], h2[:, g, c * P:(c + 1) * P], adjs[:, g, :])
                last.then_inc(sem["ZT"], 1)

            def s_mask(n):
                pe.wait_ge(sem["mrow"], n)
                pe.wait_ge(sem["x4"], n)
                for g in range(G):
                    last = mm(s[:, 3, g * N:(g + 1) * N], mrow0[:, g, :], mrow0[:, g, :])
                last.then_inc(sem["MM"], 1)

            def s_first(n):
                pe.wait_ge(sem["zt"], n)
                for o in range(C):
                    for c in range(C):
                        last = mm(s[:, 1, o * G * N:(o + 1) * G * N], g1[:, c, o * P:(o + 1) * P], zt[:, c, :],
                                  start=(c == 0), stop=(c == C - 1))
                last.then_inc(sem["Y1"], 1)

            def s_support(bank, y, ready, w, done, n):
                pe.wait_ge(sem[ready], n)
                for g in range(G):
                    for c in range(C):
                        last = mm(s[:, bank, g * D:(g + 1) * D], y[:, c, g * N:(g + 1) * N], w[:, c, :],
                                  start=(c == 0), stop=(c == C - 1))
                last.then_inc(sem[done], 1)

            def s_second(n):
                pe.wait_ge(sem["supa"], n)
                pe.wait_ge(sem["bT"], n)
                for o in range(C):
                    for g in range(G):
                        at_ = (o * G + g) * N
                        last = mm(s[:, 3, at_:at_ + N], sup[:, g, o * P:(o + 1) * P], adjs[:, g, :])
                last.then_inc(sem["Y2"], 1)

            def s_third(n):
                pe.wait_ge(sem["supb"], n)
                for g in range(G):
                    last = mm(s[:, 1, g * D:(g + 1) * D], adjs[:, g, :], sup[:, g, :])
                last.then_inc(sem["OUT"], 1)

            def s_transpose3(n):
                pe.wait_ge(sem["hn3"], n)
                transposes(s[:, 2, :], hn[3]).then_inc(sem["T_h3"], 1)

            def s_heads(kind, bank, done, n):
                for hp in range(HP):
                    a = kind * INNER + hp * P
                    o = s[:, bank + hp // 2, (hp % 2) * G * N:(hp % 2 + 1) * G * N]
                    last = chunks3(o, [(qkv_hi[:, c, a:a + P], qkv_lo[:, c, a:a + P], h3_hi[:, c, :, :], h3_lo[:, c, :, :])
                                       for c in range(C)])
                last.then_inc(sem[done], 1)

            def s_values(n):
                pe.wait_ge(sem["q"], n)
                a = 2 * INNER
                for g in range(G):
                    last = chunks3(s[:, g, :], by_node(h3_hi, h3_lo, g, lambda c: qkv_hi[:, c, a:a + INNER],
                                                       lambda c: qkv_lo[:, c, a:a + INNER]))
                last.then_inc(sem["V"], 1)

            def s_dots(g, n):
                if g == 0:
                    pe.wait_ge(sem["k_even"], n)
                    pe.wait_ge(sem["k_odd"], n)
                else:
                    pe.wait_ge(sem["v"], n)
                for b in range(2):
                    bank = s[:, BANKS[g] + b, :]
                    mm(bank, mrow[:, g, :], mbig[:, g, :].unsqueeze(1).broadcast_to([P, 4, N]), stop=False,
                       skip_group_check=True)
                    for i in range(2):
                        hp = 2 * b + i
                        last = mm(bank[:, i * 2 * N:(i + 1) * 2 * N], qT[:, hp, g, :], kbd[:, hp, g, :, :], start=False,
                                  skip_group_check=True)
                last.then_inc(sem[f"dots{g}"], 1)

            def s_transpose_p(g, n):
                pe.wait_ge(sem[f"pn{g}"], n)
                for h in range(HEADS):
                    last = pe.transpose(s[:, BANKS[g] + h // 4, (h % 4) * N:(h % 4 + 1) * N], pn[:, g, h, :], ident[:, :])
                last.then_inc(sem[f"PT{g}"], 1)

            def s_attend(g, n):
                pe.wait_ge(sem[f"at{g}"], n)
                for hp in range(HP):
                    for e in range(2):
                        h = 2 * hp + e
                        last = mm(s[e * DH:(e + 1) * DH, BANKS[g], hp * N:(hp + 1) * N], v[:, g, h * DH:(h + 1) * DH],
                                  at[:, g, h, :])
                last.then_inc(sem[f"PV{g}"], 1)

            def s_project(n):
                for g in range(G):
                    pe.wait_ge(sem[f"ot{g}"], n)
                    for hp in range(HP):
                        last = mm(s[:, 3, g * D:(g + 1) * D], ot[:, g, hp, :], wout[:, hp, :],
                                  start=(hp == 0), stop=(hp == HP - 1))
                last.then_inc(sem["W"], 1)

            pe.wait_ge(sem["id_set"], 1)
            pe.wait_ge(sem["w_split"], 1)
            pe.wait_ge(sem["pad2_set"], 1)
            pe.wait_ge(sem["pad_set"], 1)
            f_transpose(1, None)
            f_products0(1)
            f_hop1(1)
            f_trT(1)
            f_aggregate(0, s2, "s2", "A0", 1)
            f_hop0(1)
            f_aggregate(2, s1, "s1", "B0", 1)
            f_transpose1(1)
            f_products1(1)
            f_attend1(1)
            pe.wait_ge(sem["w_ready"], 1)
            pe.wait_ge(sem["w_in3"], 16 * 8)
            with pe.Fori(1, PAIRS) as t:
                s_aggregate_h(t)
                s_first(t)
                s_mask(t)
                f_transpose(t + 1, t)
                s_support(2, y1, "y1", g2, "SA", t)
                f_products0(t + 1)
                s_second(t)
                f_hop1(t + 1)
                s_support(0, y2, "y2", g3, "SB", t)
                f_trT(t + 1)
                s_third(t)
                f_aggregate(0, s2, "s2", "A0", t + 1)
                f_hop0(t + 1)
                f_aggregate(2, s1, "s1", "B0", t + 1)
                s_transpose3(t)
                pe.wait_ge(sem["h3_lo"], t)
                s_heads(0, 0, "Q", t)
                s_heads(1, 2, "K", t)
                f_transpose1(t + 1)
                s_values(t)
                s_dots(0, t)
                f_products1(t + 1)
                s_dots(1, t)
                f_attend1(t + 1)
                s_transpose_p(0, t)
                s_transpose_p(1, t)
                s_attend(0, t)
                s_attend(1, t)
                s_project(t)
            n = PAIRS
            s_aggregate_h(n)
            s_first(n)
            s_mask(n)
            s_support(2, y1, "y1", g2, "SA", n)
            s_second(n)
            s_support(0, y2, "y2", g3, "SB", n)
            s_third(n)
            s_transpose3(n)
            pe.wait_ge(sem["h3_lo"], n)
            s_heads(0, 0, "Q", n)
            s_heads(1, 2, "K", n)
            s_values(n)
            s_dots(0, n)
            s_dots(1, n)
            s_transpose_p(0, n)
            s_transpose_p(1, n)
            s_attend(0, n)
            s_attend(1, n)
            s_project(n)


_INS = ["x", "adj", "nodemask", "L0_gnn_Wv", "L0_gnn_bv", "L0_gnn_aw", "L0_gnn_ab", "L0_gnn_Wk", "L0_gnn_bk",
        "L1_gnn_W", "L1_gnn_a", "L2_gnn_W1", "L2_gnn_b1", "L2_gnn_W2", "L2_gnn_b2", "L2_gnn_W3", "L2_gnn_b3",
        "L3_gnn_W_qkv", "L3_gnn_W_out", "L3_gnn_b_out"]


def kernel(**inputs):
    import numpy as _np
    import concourse.bacc as _bacc
    from concourse import mybir as _mybir
    from concourse.bass_utils import run_bass_kernel_spmd as _run

    nc = _bacc.Bacc("TRN2", target_bir_lowering=False, num_devices=1)
    arrays, args = {}, []
    for name in _INS:
        a = _np.ascontiguousarray(inputs[name])
        if a.dtype == bool:
            a = a.view(_np.uint8)
        arrays[f"in_{name}"] = a
        args.append(nc.dram_tensor(f"in_{name}", a.shape, _mybir.dt.from_np(a.dtype), kind="ExternalInput").ap())
    shape = inputs["x"].shape
    args.append(nc.dram_tensor("out_x", shape, _mybir.dt.float32, kind="ExternalOutput").ap())
    build(nc, *args)
    r = _run(nc, [arrays], core_ids=[0])
    return r.results[0]["out_x"]
```

```python
import concourse.bass as bass
from concourse import mybir
from contextlib import ExitStack


def build(nc, x, adj, nodemask, l0_wv, l0_bv, l0_aw, l0_ab, l0_wk, l0_bk, l1_w, l1_a,
          l2_w1, l2_b1, l2_w2, l2_b2, l2_w3, l2_b3, l3_wqkv, l3_wout, l3_bout, out):
    fp32 = mybir.dt.float32
    f32r = mybir.dt.float32r
    bf16 = mybir.dt.bfloat16
    ALU = mybir.AluOpType
    ACT = mybir.ActivationFunctionType
    AX = mybir.AxisListType

    GRAPHS, N, D = x.shape
    P = 128
    C = D // P
    G = 2
    PAIRS = GRAPHS // G
    HEADS = 8
    DH = l3_wout.shape[0] // HEADS
    INNER = HEADS * DH
    HP = HEADS // 2
    KHOPS = l0_wk.shape[0]
    EXT = D + 2
    EPS = 1e-5
    ROW_EPS = 1e-12
    SLOPE = 0.2
    NEG_INF = -9e15
    CAP = 3e38
    BIG = 2.0 ** 127
    SCALE = float(DH) ** -0.5
    LA = LG = 0.33

    ctx = ExitStack()
    with ctx:
        def sb(name, shape, dt=fp32):
            return ctx.enter_context(nc.sbuf_tensor(name, shape, dt))

        ident = sb("ident", [P, P])
        stage = sb("stage", [P, 3 * C * INNER])
        w_raw = stage[:, :].rearrange("p (c n) -> p c n", c=C)
        stage4 = sb("stage4", [P, C * D])
        wv_raw = stage4[:, :].rearrange("p (c n) -> p c n", c=C)
        mn = sb("mn", [P, G, D])
        ex = sb("ex", [P, G, D])
        aw_bc, a_bc = mn, ex
        stage5 = sb("stage5", [P, G * INNER])
        bv_bc = stage5[:, KHOPS * D:(KHOPS + 1) * D]
        bk_bc = stage5[:, 0:KHOPS * D].rearrange("p (k n) -> p k n", k=KHOPS)
        ab_bc = sb("ab_bc", [P, 1])
        stage2 = sb("stage2", [P, 10 * D])
        junk = stage2[:, :].rearrange("p (k n) -> p k n", k=10)
        att0 = sb("att0", [P, C, 2])
        att1 = sb("att1", [P, C, 2])
        c_part = sb("c_part", [P, 3])
        c0 = sb("c0", [P, 1])
        k_hi = sb("k_hi", [P, C, KHOPS, EXT], f32r)
        k_lo = sb("k_lo", [P, C, KHOPS, EXT], f32r)
        w1_hi = sb("w1_hi", [P, C, EXT], f32r)
        w1_lo = sb("w1_lo", [P, C, EXT], f32r)
        v0_hi = sb("v0_hi", [P, C, P], f32r)
        v0_lo = sb("v0_lo", [P, C, P], f32r)
        v1_hi = sb("v1_hi", [P, C, P], f32r)
        v1_lo = sb("v1_lo", [P, C, P], f32r)
        gb1 = sb("gb1", [P, C])
        gb2 = sb("gb2", [P, C])
        b3_bc = sb("b3_bc", [P, D])
        qkv_hi = sb("qkv_hi", [P, C, 3 * INNER], f32r)
        qkv_lo = sb("qkv_lo", [P, C, 3 * INNER], f32r)
        stage3 = sb("stage3", [P, G * HEADS * N])
        wout = stage3[:, 0:HP * D].rearrange("p (h n) -> p h n", h=HP)
        g1 = stage3[:, HP * D:(HP + C) * D].rearrange("p (c n) -> p c n", c=C)
        wout_hi = sb("wout_hi", [P, HP, D], f32r)
        wout_lo = sb("wout_lo", [P, HP, D], f32r)
        g2 = stage3[:, (HP + C) * D:(HP + 2 * C) * D].rearrange("p (c n) -> p c n", c=C)
        x2b = sb("x2b", [P, G, D])
        g3 = x2b
        g2_hi = sb("g2_hi", [P, C, D], f32r)
        g2_lo = sb("g2_lo", [P, C, D], f32r)
        g3_hi = sb("g3_hi", [P, C, D], f32r)
        g3_lo = sb("g3_lo", [P, C, D], f32r)
        g1_hi = sb("g1_hi", [P, C, D], f32r)
        g1_lo = sb("g1_lo", [P, C, D], f32r)
        bout_bc = sb("bout_bc", [P, D])
        bsum = sb("bsum", [P, D])
        bsum_a = sb("bsum_a", [P, D])
        spare = sb("spare", [P, 1])
        zero = sb("zero", [P, 1])
        expo = sb("expo", [P, G])

        x0 = sb("x0", [P, G, D])
        xr = sb("xr", [P, G, D])
        adj_ij = sb("adj_ij", [P, G, N])
        mask_u8 = sb("mask_u8", [1, G * N], mybir.dt.uint8)
        stats = [sb(f"stats{k}", [P, G, 6]) for k in range(4)]
        mv = [sb(f"mv{k}", [P, G, 2]) for k in range(4)]
        veps = [sb(f"veps{k}", [P, G]) for k in range(4)]
        rstd = [sb(f"rstd{k}", [P, G]) for k in range(4)]
        hn = [sb(f"hn{k}", [P, G, D]) for k in range(4)]
        h2 = sb("h2", [P, G, D])
        h0_hi = sb("h0_hi", [P, C, G, N], f32r)
        h0_lo = sb("h0_lo", [P, C, G, N], f32r)
        h1_hi = sb("h1_hi", [P, C, G, N], f32r)
        h1_lo = sb("h1_lo", [P, C, G, N], f32r)
        h3_hi = sb("h3_hi", [P, C, G, N], f32r)
        h3_lo = sb("h3_lo", [P, C, G, N], f32r)
        adj_ji = sb("adj_ji", [P, G, N])
        adjs = sb("adjs", [P, G, N])
        sic = sb("sic", [P, G])
        z0 = sb("z0", [P, G, N])
        l0 = sb("l0", [P, G, N])
        e0 = sb("e0", [P, G, N])
        alpha = sb("alpha", [P, G, N])
        rsum = sb("rsum", [P, G])
        rsume = sb("rsume", [P, G])
        rinv = sb("rinv", [P, G])
        tr = sb("tr", [P, G, N])
        trT = sb("trT", [P, G, N])
        s2 = sb("s2", [P, G, D + 1])
        s1 = sb("s1", [P, G, D])
        xt = sb("xt", [P, G, D])
        x1 = sb("x1", [P, G, D])
        cap = sb("cap", [P, G, N])
        wh2 = sb("wh2", [P, G])
        z1 = sb("z1", [P, G, N])
        l1 = sb("l1", [P, G, N])
        em = sb("em", [P, G, N])
        nmax1 = sb("nmax1", [P, G])
        p1 = sb("p1", [P, G, N])
        den1 = sb("den1", [P, G])
        rden1 = sb("rden1", [P, G])
        whs = sb("whs", [P, G, D])
        rx = sb("rx", [P, G, D])
        x2 = sb("x2", [P, G, D])
        zt_hi = sb("zt_hi", [P, C, G * N], f32r)
        zt_lo = sb("zt_lo", [P, C, G * N], f32r)
        y = sb("y", [P, C, G * N])
        y_hi = sb("y_hi", [P, C, G * N], f32r)
        y_lo = sb("y_lo", [P, C, G * N], f32r)
        sup = sb("sup", [P, G, D])
        x3 = sb("x3", [P, G, D])
        x3b = sb("x3b", [P, G, D])
        mrow = sb("mrow", [P, G, N], bf16)
        mrow0 = sb("mrow0", [P, G, N], bf16)
        mbig = sb("mbig", [P, G, N], bf16)
        ed = sb("ed", [P, G, N])
        bd = sb("bd", [P, G, N])
        bT = sb("bT", [P, G, N])
        qT = sb("qT", [P, HP, G, N])
        kbd = sb("kbd", [P, HP, G, 2, N])
        v = stage5[:, :].rearrange("p (g n) -> p g n", g=G)
        nm = sb("nm", [P, G, HEADS])
        rs = sb("rs", [P, G, HEADS])
        ri = sb("ri", [P, G, HEADS])
        pr = stage[:, 0:G * HEADS * N].rearrange("p (g h n) -> p g h n", g=G, h=HEADS)
        pn = stage3[:, :].rearrange("p (g h n) -> p g h n", g=G, h=HEADS)
        at = stage2[:, 0:G * HEADS * N].rearrange("p (g h n) -> p g h n", g=G, h=HEADS)
        ot_hi = sb("ot_hi", [P, G, HP, N], f32r)
        ot_lo = sb("ot_lo", [P, G, HP, N], f32r)
        x4 = stage4[:, :].rearrange("p (g n) -> p g n", g=G)

        f = ctx.enter_context(nc.psum_tensor("f", [P, 4, 512], fp32))
        s_banks = ctx.enter_context(nc.psum_tensor("s_banks", [P, 4, 512], fp32))

        HALF = HEADS // 2
        BANKS = (2, 3, 0, 1)

        def half(tile, q):
            return tile[:, q // 2, HALF * (q % 2):HALF * (q % 2 + 1)]

        names = """
            w_in w_in2 w_in3 w_junk w_att w_c w_c0 w_bsa w_split w_ready pad_set pad2_set id_zero id_set
            mask_pad expo_set x_in adj_in mask_in out_done T_h0 T_adj xr adjT h0_hi h0_lo E0 S2p si z0 l0 e0
            alpha rsume rinv tr TT trT s2 A0 s1 B0 xt x1 T_h1 h1_hi h1_lo Wh cap wh2 z1 l1 em nmax1 p1 rden1 whs
            Hp mn ex rx x2 h2 adjs x2b ZT MM zt_hi zt_lo Y1 y1_hi y1 y1_lo SA supa Y2 y2_hi y2 y2_lo SB supb OUT
            x3 x3b ed bd bT T_h3 h3_hi h3_lo Q q K k_even k_odd V v mrow PV0 PV1 ot0_hi ot1_hi ot0_lo ot1_lo W
            x4 w_g1""".split()
        sem = {n: ctx.enter_context(nc.semaphore(n)) for n in names}
        for k in range(4):
            for n in ("stats", "mv", "veps", "rstd", "hn", "dots", "nm", "pr", "ri", "pn", "PT", "at"):
                sem[f"{n}{k}"] = ctx.enter_context(nc.semaphore(f"{n}_{k}"))

        block = ctx.enter_context(nc.Block())

        def pair_rows(a, t):
            if isinstance(t, int):
                return a[t * G:(t + 1) * G].rearrange("g n d -> n g d")
            return a[bass.ds(t * G, G)].rearrange("g n d -> n g d")

        def pair_mask(start):
            m = nodemask.rearrange("(a g) n -> a (g n)", a=1)
            return m[:, start:start + G * N] if isinstance(start, int) else m[:, bass.ds(start, G * N)]

        def per_graph(b):
            return b[:, :].unsqueeze(1).broadcast_to([P, G, D])

        LOADS1 = 11 + 2 * KHOPS
        LOADS2 = 3 * C

        @block.sync
        def _(sp):
            def row_bc(a, width):
                return a.rearrange("(a n) -> a n", a=1).broadcast_to([P, width])

            def load(t):
                sp.dma_start(x0[:, :, :], pair_rows(x, t)).then_inc(sem["x_in"], 16)
                sp.dma_start(adj_ij[:, :, :], pair_rows(adj, t)).then_inc(sem["adj_in"], 16)

            def load_mask(start):
                sp.dma_start(mask_u8[:, :], pair_mask(start)).then_inc(sem["mask_in"], 16)

            load(0)
            load_mask(0)
            n1 = [sp.dma_start(wv_raw[:, :, :], l0_wv.rearrange("(c p) n -> p c n", c=C)),
                  sp.dma_start(w_raw[:, :, 3 * D:4 * D], l1_w.rearrange("(c p) n -> p c n", c=C)),
                  sp.dma_start(bv_bc[:, :], row_bc(l0_bv, D)),
                  sp.dma_start(ab_bc[:, :], row_bc(l0_ab, 1))]
            for j in range(2):
                n1.append(sp.dma_start(aw_bc[:, j, :], row_bc(l0_aw[j * D:(j + 1) * D, :].rearrange("n a -> (n a)"), D)))
                n1.append(sp.dma_start(a_bc[:, j, :], row_bc(l1_a[j * D:(j + 1) * D, :].rearrange("n a -> (n a)"), D)))
            for k in range(KHOPS):
                n1.append(sp.dma_start(w_raw[:, :, k * D:(k + 1) * D], l0_wk[k].rearrange("(c p) n -> p c n", c=C)))
                n1.append(sp.dma_start(bk_bc[:, k, :], row_bc(l0_bk[k], D)))
            for d in n1:
                d.then_inc(sem["w_in"], 16)
            assert len(n1) == LOADS1 - 3
            n3 = [sp.dma_start(g[:, :, :], w.rearrange("(c p) n -> p c n", c=C))
                  for g, w in ((g1, l2_w1), (g2, l2_w2), (g3, l2_w3))]
            n3 += [sp.dma_start(g[:, :], b.rearrange("(c p) -> p c", c=C), allow_slow_non_contiguous=True) for g, b in ((gb1, l2_b1), (gb2, l2_b2))]
            n3 += [sp.dma_start(b3_bc[:, :], row_bc(l2_b3, D)), sp.dma_start(bout_bc[:, :], row_bc(l3_bout, D)),
                   sp.dma_start(wout[:, :, :], l3_wout.rearrange("(c p) n -> p c n", c=HP))]
            for d in n3:
                d.then_inc(sem["w_in3"], 16)
            sp.wait_ge(sem["w_split"], 1)
            for c in range(C):
                for kind in range(3):
                    src = l3_wqkv[c * P:(c + 1) * P, :].rearrange("p (h k d) -> p h k d", h=HEADS, k=3)[:, :, kind, :]
                    dst = w_raw[:, c, kind * INNER:(kind + 1) * INNER].rearrange("p (h d) -> p h d", h=HEADS)
                    sp.dma_start(dst, src).then_inc(sem["w_in2"], 16)

            def load_adj(t, n):
                sp.wait_ge(sem["tr"], n)
                sp.wait_ge(sem["T_adj"], n)
                sp.dma_start(adj_ij[:, :, :], pair_rows(adj, t)).then_inc(sem["adj_in"], 16)

            def load_x(t, n):
                sp.wait_ge(sem["xr"], n)
                sp.wait_ge(sem["T_h0"], n)
                sp.dma_start(x0[:, :, :], pair_rows(x, t)).then_inc(sem["x_in"], 16)

            def store(t, n):
                sp.wait_ge(sem["x4"], n + 1)
                sp.dma_start(pair_rows(out, t), x4[:, :, :]).then_inc(sem["out_done"], 16)

            load_x(1, 1)
            load_adj(1, 1)
            sp.sem_inc(sem["out_done"], 16)
            sp.sem_inc(sem["x4"], 1)
            load_x(2, 2)
            load_adj(2, 2)
            sp.wait_ge(sem["mrow"], 1)
            load_mask(G * N)
            with sp.Fori(1, PAIRS - 2) as t:
                load_x(t + 2, t + 2)
                load_adj(t + 2, t + 2)
                sp.wait_ge(sem["mrow"], t + 1)
                load_mask(t * (G * N) + G * N)
                store(t - 1, t)
            sp.wait_ge(sem["mrow"], PAIRS - 1)
            load_mask((PAIRS - 1) * G * N)
            store(PAIRS - 3, PAIRS - 2)
            store(PAIRS - 2, PAIRS - 1)
            store(PAIRS - 1, PAIRS)
            sp.wait_ge(sem["out_done"], 16 * (PAIRS + 1))

        @block.gpsimd
        def _(gp):
            gp.memset(zero[:, :], 0.0)
            gp.memset(expo[:, :], -0.5).then_inc(sem["expo_set"], 1)
            gp.memset(ident[:, :], 0.0).then_inc(sem["id_zero"], 1)
            gp.wait_ge(sem["id_zero"], 1)
            gp.affine_select(out=ident[:, :], in_=ident[:, :], compare_op=ALU.not_equal, fill=1.0,
                             base=0, pattern=[[-1, P]], channel_multiplier=1).then_inc(sem["id_set"], 1)
            gp.memset(kbd[:, :, :, :, :], 0.0).then_inc(sem["pad_set"], 1)
            gp.wait_ge(sem["expo_set"], 1)
            gp.wait_ge(sem["w_in3"], 16 * 8)

            def power(k, n):
                gp.wait_ge(sem[f"veps{k}"], n)
                gp.tensor_tensor(rstd[k][:, :], veps[k][:, :], expo[:, :], ALU.pow).then_inc(sem[f"rstd{k}"], 1)

            def distance(n):
                gp.wait_ge(sem["ed"], n)
                gp.tensor_tensor(bd[:, :, :], adjs[:, :, :], ed[:, :, :], ALU.add).then_inc(sem["bd"], 1)

            def x3_bias(n):
                gp.wait_ge(sem["x3"], n * G)
                gp.tensor_tensor(x3b[:, :, :], x3[:, :, :], per_graph(bout_bc), ALU.add).then_inc(sem["x3b"], 1)

            def probs(q, n):
                gp.wait_ge(sem[f"ri{q}"], n)
                gp.tensor_tensor(half(pn, q), half(pr, q), half(ri, q).unsqueeze(2).broadcast_to([P, HALF, N]), ALU.mult)\
                    .then_inc(sem[f"pn{q}"], 1)

            def copy_adj(f1, s):
                if s is not None:
                    gp.wait_ge(sem["bT"], s)
                    gp.wait_ge(sem["OUT"], s * G)
                gp.wait_ge(sem["adjT"], f1)
                gp.tensor_tensor(adjs[:, :, :], adj_ji[:, :, :], zero[:, :].unsqueeze(2).broadcast_to([P, G, N]), ALU.add)\
                    .then_inc(sem["adjs"], 1)

            def x2_bias(f1, s):
                if s is not None:
                    gp.wait_ge(sem["x3"], s * G)
                gp.wait_ge(sem["x2"], f1)
                gp.tensor_tensor(x2b[:, :, :], x2[:, :, :], per_graph(b3_bc), ALU.add).then_inc(sem["x2b"], 1)

            def turn(fn, f1, s):
                if f1 is not None:
                    power(1, f1)
                    copy_adj(f1, s)
                if s is not None:
                    power(3, s)
                    x3_bias(s)
                if f1 is not None:
                    distance(f1)
                    power(2, f1)
                    x2_bias(f1, s)
                if s is not None:
                    for q in range(4):
                        probs(q, s)
                if fn is not None:
                    power(0, fn)

            turn(1, None, None)
            turn(2, None, None)
            turn(3, 1, None)
            with gp.Fori(1, PAIRS - 2) as t:
                turn(t + 3, t + 1, t)
            turn(None, PAIRS - 1, PAIRS - 2)
            turn(None, PAIRS, PAIRS - 1)
            turn(None, None, PAIRS)

        @block.scalar
        def _(act):
            def copy(o, i):
                return act.activation(o, i, ACT.Copy)

            def f_x_copy(n, f1):
                act.wait_ge(sem["x_in"], 16 * n)
                if f1 is not None:
                    act.wait_ge(sem["x1"], f1)
                copy(xr[:, :, :], x0[:, :, :]).then_inc(sem["xr"], 1)

            def f_h0(n, f1):
                act.wait_ge(sem["T_h0"], n)
                act.activation(h0_hi[:, :, :, :], f[:, 0, :], ACT.Relu).then_inc(sem["h0_hi"], 1)

            def f_adj(n, f1):
                act.wait_ge(sem["T_adj"], n)
                if f1 is not None:
                    act.wait_ge(sem["cap"], f1)
                    act.wait_ge(sem["adjs"], f1)
                copy(adj_ji[:, :, :], f[:, 1, 0:G * N]).then_inc(sem["adjT"], 1)

            def f_s2(n):
                act.wait_ge(sem["S2p"], n)
                copy(s2[:, :, :], f[:, 2:4, 0:D + 1]).then_inc(sem["s2"], 1)

            def f_exp0(n):
                act.wait_ge(sem["l0"], n)
                act.activation(e0[:, :, :], l0[:, :, :], ACT.Exp).then_inc(sem["e0"], 1)

            def f_trT(n):
                act.wait_ge(sem["TT"], n)
                copy(trT[:, :, :], f[:, 1, 0:G * N]).then_inc(sem["trT"], 1)

            def f_s1(n):
                act.wait_ge(sem["A0"], n)
                copy(s1[:, :, :], f[:, 0, :]).then_inc(sem["s1"], 1)

            def f_h1(n):
                act.wait_ge(sem["T_h1"], n)
                act.activation(h1_hi[:, :, :, :], s_banks[:, 2, :], ACT.Relu).then_inc(sem["h1_hi"], 1)

            def f_att1(n):
                act.wait_ge(sem["nmax1"], n)
                for g in range(G):
                    p = act.activation(p1[:, g, :], em[:, g, :], ACT.Exp, bias=nmax1[:, g:g + 1],
                                       accum_out=den1[:, g:g + 1])
                p.then_inc(sem["p1"], 1)

            def f_scaled(n):
                act.wait_ge(sem["rden1"], n)
                for g in range(G):
                    w = act.activation(whs[:, g, :], f[:, 2 + g, 0:D], ACT.Copy, scale=rden1[:, g:g + 1])
                w.then_inc(sem["whs"], 1)

            def f_elu(n):
                act.wait_ge(sem["mn"], n)
                act.activation(ex[:, :, :], mn[:, :, :], ACT.Exp).then_inc(sem["ex"], 1)

            def f_zt(n):
                act.wait_ge(sem["ZT"], n)
                copy(zt_hi[:, :, :], f[:, 1, :]).then_inc(sem["zt_hi"], 1)

            def f_exp_adj(n):
                act.wait_ge(sem["adjs"], n)
                act.activation(ed[:, :, :], adjs[:, :, :], ACT.Exp, scale=-1.0).then_inc(sem["ed"], 1)

            def s_relu(made, bank, bias, done, n):
                act.wait_ge(sem[made], n)
                for tile, name in ((y_hi, f"{done}_hi"), (y, done)):
                    for c in range(C):
                        r = act.activation(tile[:, c, :], bank[:, c * G * N:(c + 1) * G * N], ACT.Relu, bias=bias[:, c:c + 1])
                    r.then_inc(sem[name], 1)

            def s_sup(made, bank, done, n):
                act.wait_ge(sem[made], n)
                copy(sup[:, :, :], s_banks[:, bank, :]).then_inc(sem[done], 1)

            def s_h3(n):
                act.wait_ge(sem["T_h3"], n)
                for c in range(C):
                    act.activation(h3_hi[:, c, :, :], s_banks[:, 2, c * G * N:(c + 1) * G * N], ACT.Relu)\
                        .then_inc(sem["h3_hi"], 1)

            def s_q(n):
                act.wait_ge(sem["Q"], n)
                act.activation(qT[:, :, :, :], s_banks[:, 0:2, :], ACT.Copy, scale=SCALE).then_inc(sem["q"], 1)

            def s_k_even(n):
                act.wait_ge(sem["K"], n)
                copy(kbd[0:DH, :, :, 0, :], s_banks[0:DH, 2:4, :].rearrange("p b (q n) -> p (b q) n", n=N))\
                    .then_inc(sem["k_even"], 1)

            def s_v(n):
                act.wait_ge(sem["V"], n)
                copy(v[:, :, :], s_banks[:, 0:2, :]).then_inc(sem["v"], 1)

            def s_exps(q, n):
                act.wait_ge(sem[f"nm{q}"], n)
                for i in range(HALF):
                    e = act.activation(half(pr, q)[:, i, :], s_banks[:, BANKS[q], i * N:(i + 1) * N], ACT.Exp,
                                       bias=half(nm, q)[:, i:i + 1], accum_out=half(rs, q)[:, i:i + 1])
                e.then_inc(sem[f"pr{q}"], 1)

            def s_ot(g, n):
                act.wait_ge(sem[f"PV{g}"], n)
                copy(ot_hi[:, g, :, :], s_banks[:, BANKS[2 * g], :]).then_inc(sem[f"ot{g}_hi"], 1)

            def turn(f0, f1, s):
                if s is not None:
                    s_sup("SA", 2, "supa", s)
                if f0 is not None:
                    f_h0(f0, f1)
                    f_x_copy(f0, f1)
                if s is not None:
                    s_relu("Y2", s_banks[:, 3, :], gb2, "y2", s)
                if f0 is not None:
                    f_s2(f0)
                if s is not None:
                    s_sup("SB", 1, "supb", s)
                if f1 is not None:
                    f_h1(f1)
                if f0 is not None:
                    f_exp0(f0)
                if f1 is not None:
                    f_exp_adj(f1)
                if s is not None:
                    s_h3(s)
                if f1 is not None:
                    f_att1(f1)
                if s is not None:
                    s_q(s)
                if f0 is not None:
                    f_adj(f0, f1)
                if f1 is not None:
                    f_scaled(f1)
                if s is not None:
                    s_k_even(s)
                if f1 is not None:
                    f_elu(f1)
                if s is not None:
                    s_v(s)
                if f0 is not None:
                    f_trT(f0)
                if s is not None:
                    for q in range(4):
                        s_exps(q, s)
                if f1 is not None:
                    f_zt(f1)
                if s is not None:
                    s_ot(0, s)
                if f1 is not None:
                    s_relu("Y1", f[:, 3, :], gb1, "y1", f1)
                if f0 is not None:
                    f_s1(f0)
                if s is not None:
                    s_ot(1, s)

            act.wait_ge(sem["w_in3"], 16 * 8)
            turn(1, None, None)
            turn(2, 1, None)
            with act.Fori(1, PAIRS - 1) as t:
                turn(t + 2, t + 1, t)
            turn(None, PAIRS, PAIRS - 1)
            turn(None, None, PAIRS)

        @block.vector
        def _(dve):
            dve.wait_ge(sem["w_in"], 16 * (LOADS1 - 3))
            wl1 = w_raw[:, :, 3 * D:4 * D]
            k = 0
            for c in range(C):
                for j in range(2):
                    dve.tensor_tensor_reduce(out=junk[:, k, :], in0=wv_raw[:, c, :], in1=aw_bc[:, j, :], scale=1.0,
                                             scalar=0.0, op0=ALU.mult, op1=ALU.add, accum_out=att0[:, c, j:j + 1])
                    dve.tensor_tensor_reduce(out=junk[:, k + 1, :], in0=wl1[:, c, :], in1=a_bc[:, j, :], scale=1.0,
                                             scalar=0.0, op0=ALU.mult, op1=ALU.add, accum_out=att1[:, c, j:j + 1])
                    k += 2
            for j in range(2):
                last = dve.tensor_tensor_reduce(out=junk[:, k + j, :], in0=bv_bc[:, :], in1=aw_bc[:, j, :], scale=1.0,
                                                scalar=0.0, op0=ALU.mult, op1=ALU.add, accum_out=c_part[:, j:j + 1])
            last.then_inc(sem["w_att"], 1)
            dve.wait_ge(sem["w_att"], 1)
            dve.tensor_tensor(c_part[:, 2:3], c_part[:, 0:1], c_part[:, 1:2], ALU.add).then_inc(sem["w_c"], 1)
            dve.tensor_tensor(bsum_a[:, :], bk_bc[:, 0, :], bk_bc[:, 1, :], ALU.add).then_inc(sem["w_bsa"], 1)
            dve.wait_ge(sem["w_c"], 1)
            dve.tensor_tensor(c0[:, :], c_part[:, 2:3], ab_bc[:, :], ALU.add).then_inc(sem["w_c0"], 1)
            dve.wait_ge(sem["w_bsa"], 1)
            dve.tensor_tensor(bsum[:, :], bsum_a[:, :], bk_bc[:, 2, :], ALU.add)
            zero_col = [(k_hi, k_lo), (w1_hi, w1_lo)]
            for hi, lo in zero_col:
                for w in (hi, lo):
                    tail = w[:, :, :, D + 1:EXT] if w in (k_hi, k_lo) else w[:, :, D + 1:EXT]
                    last = dve.memset(tail.bitcast(fp32), 0.0)
            last.then_inc(sem["pad2_set"], 1)

            def hi_part(hi, full):
                return dve.tensor_copy(hi, full)

            def lo_part(lo, full, hi):
                return dve.tensor_tensor(lo, full, hi.bitcast(fp32), ALU.subtract)

            cols0 = [(k_hi[:, :, j, 0:D], k_lo[:, :, j, 0:D], w_raw[:, :, j * D:(j + 1) * D]) for j in range(KHOPS)]
            cols1 = [(k_hi[:, :, j, D:D + 1], k_lo[:, :, j, D:D + 1], att0[:, :, 1:2]) for j in range(KHOPS)]
            cols2 = [(w1_hi[:, :, 0:D], w1_lo[:, :, 0:D], wl1), (w1_hi[:, :, D:D + 1], w1_lo[:, :, D:D + 1], att1[:, :, 1:2])]
            cols3 = [(v0_hi[:, :, :], v0_lo[:, :, :], att0[:, :, 0:1].broadcast_to([P, C, P])),
                     (v1_hi[:, :, :], v1_lo[:, :, :], att1[:, :, 0:1].broadcast_to([P, C, P]))]
            parts = cols0 + cols1 + cols2 + cols3
            for hi, lo, full in parts:
                last = hi_part(hi, full)
            last.then_inc(sem["w_junk"], 1)
            dve.wait_ge(sem["w_junk"], 1)
            for hi, lo, full in parts:
                last = lo_part(lo, full, hi)
            last.then_inc(sem["w_split"], 1)
            dve.memset(mrow0[:, :, :], 0.0)
            dve.memset(mrow[:, :, :], 0.0)
            dve.memset(mbig[:, :, :], 0.0).then_inc(sem["mask_pad"], 1)
            dve.wait_ge(sem["mask_pad"], 1)
            dve.memset(mrow[0:2, :, :], 1.0)
            dve.memset(mbig[0:2, :, :], -BIG).then_inc(sem["mask_pad"], 1)
            dve.wait_ge(sem["w_in3"], 16 * 8)
            for hi, full in ((g1_hi, g1), (g2_hi, g2), (g3_hi, g3)):
                hi_part(hi[:, :, :], full[:, :, :])
            hi_part(wout_hi[:, :, :], wout[:, :, :]).then_inc(sem["w_junk"], 1)
            dve.wait_ge(sem["w_junk"], 2)
            for lo, full, hi in ((g1_lo, g1, g1_hi), (g2_lo, g2, g2_hi), (g3_lo, g3, g3_hi)):
                lo_part(lo[:, :, :], full[:, :, :], hi[:, :, :])
            lo_part(wout_lo[:, :, :], wout[:, :, :], wout_hi[:, :, :]).then_inc(sem["w_g1"], 1)
            dve.wait_ge(sem["w_in2"], 16 * LOADS2)
            hi_part(qkv_hi[:, :, :], w_raw[:, :, :]).then_inc(sem["w_junk"], 1)
            dve.wait_ge(sem["w_junk"], 3)
            lo_part(qkv_lo[:, :, :], w_raw[:, :, :], qkv_hi[:, :, :]).then_inc(sem["w_ready"], 1)
            dve.wait_ge(sem["mask_pad"], 2)

            def norm_stats(k, src, n, by_graph=None):
                for g in range(G):
                    if by_graph is not None:
                        dve.wait_ge(by_graph, n * G - (G - 1 - g))
                    b = dve.bn_stats(stats[k][:, g, :], src[:, g, :])
                b.then_inc(sem[f"stats{k}"], 1)
                dve.wait_ge(sem[f"stats{k}"], n)
                dve.memset(spare[:, :], 0.0)
                for g in range(G):
                    b = dve.bn_aggr(mv[k][:, g, :], stats[k][:, g, :])
                b.then_inc(sem[f"mv{k}"], 1)
                dve.wait_ge(sem[f"mv{k}"], n)
                dve.tensor_scalar(veps[k][:, :], mv[k][:, :, 1], EPS, None, ALU.add).then_inc(sem[f"veps{k}"], 1)

            def norm_apply(k, src, n):
                dve.wait_ge(sem[f"rstd{k}"], n)
                for g in range(G):
                    dve.tensor_scalar(hn[k][:, g, :], src[:, g, :], mv[k][:, g, 0:1], rstd[k][:, g:g + 1],
                                      ALU.subtract, ALU.mult).then_inc(sem[f"hn{k}"], 1)

            def lo_relu(k, bank, hi, lo, n):
                dve.wait_ge(sem[f"h{k}_hi"], n * C if k == 3 else n)
                dve.scalar_tensor_tensor(lo[:, :, :, :].rearrange("p c g n -> p (c g n)"), bank, 0.0,
                                         hi[:, :, :, :].bitcast(fp32).rearrange("p c g n -> p (c g n)"),
                                         ALU.max, ALU.subtract).then_inc(sem[f"h{k}_lo"], 1)

            def f_norm0(n):
                dve.wait_ge(sem["x_in"], 16 * n)
                norm_stats(0, x0, n)

            def f_si(n):
                dve.wait_ge(sem["s2"], n)
                dve.tensor_scalar(sic[:, :], s2[:, :, D], c0[:, 0:1], None, ALU.add).then_inc(sem["si"], 1)

            def f_logits0(n):
                dve.wait_ge(sem["E0"], n)
                dve.wait_ge(sem["si"], n)
                for g in range(G):
                    z = dve.tensor_scalar(z0[:, g, :], s_banks[:, 3, g * N:(g + 1) * N], sic[:, g:g + 1], None, ALU.add)
                z.then_inc(sem["z0"], 1)
                dve.wait_ge(sem["z0"], n)
                dve.scalar_tensor_tensor(l0[:, :, :], z0[:, :, :], SLOPE, z0[:, :, :], ALU.mult, ALU.max)\
                    .then_inc(sem["l0"], 1)

            def f_transition(n):
                dve.wait_ge(sem["e0"], n)
                dve.wait_ge(sem["adj_in"], 16 * n)
                for g in range(G):
                    a = dve.tensor_tensor_reduce(out=alpha[:, g, :], in0=e0[:, g, :], in1=adj_ij[:, g, :], scale=1.0,
                                                 scalar=0.0, op0=ALU.mult, op1=ALU.add, accum_out=rsum[:, g:g + 1])
                a.then_inc(sem["alpha"], 1)
                dve.wait_ge(sem["alpha"], n)
                dve.tensor_scalar(rsume[:, :], rsum[:, :], ROW_EPS, None, ALU.add).then_inc(sem["rsume"], 1)
                dve.wait_ge(sem["rsume"], n)
                dve.reciprocal(rinv[:, :], rsume[:, :]).then_inc(sem["rinv"], 1)
                dve.wait_ge(sem["rinv"], n)
                for g in range(G):
                    a = dve.tensor_scalar(tr[:, g, :], alpha[:, g, :], rinv[:, g:g + 1], None, ALU.mult)
                a.then_inc(sem["tr"], 1)

            def f_x1(n):
                dve.wait_ge(sem["B0"], n)
                dve.tensor_tensor(xt[:, :, :], f[:, 2, :].rearrange("p (g d) -> p g d", g=G), per_graph(bsum), ALU.add)\
                    .then_inc(sem["xt"], 1)
                dve.wait_ge(sem["xt"], n)
                dve.wait_ge(sem["xr"], n)
                dve.scalar_tensor_tensor(x1[:, :, :], xt[:, :, :], 0.0, xr[:, :, :], ALU.max, ALU.add)\
                    .then_inc(sem["x1"], 1)

            def f_cap(n):
                dve.wait_ge(sem["adjT"], n)
                dve.tensor_scalar(cap[:, :, :], adj_ji[:, :, :], 0.5, CAP, ALU.is_gt, ALU.mult).then_inc(sem["cap"], 1)

            def f_logits1(n):
                dve.wait_ge(sem["Wh"], n)
                dve.tensor_copy(wh2[:, :], f[:, 2:4, D]).then_inc(sem["wh2"], 1)
                dve.wait_ge(sem["wh2"], n)
                for g in range(G):
                    z = dve.tensor_scalar(z1[:, g, :], f[:, 1, g * N:(g + 1) * N], wh2[:, g:g + 1], None, ALU.add)
                z.then_inc(sem["z1"], 1)

            def f_maxima1(n):
                dve.wait_ge(sem["z1"], n)
                dve.scalar_tensor_tensor(l1[:, :, :], z1[:, :, :], SLOPE, z1[:, :, :], ALU.mult, ALU.max)\
                    .then_inc(sem["l1"], 1)
                dve.wait_ge(sem["l1"], n)
                dve.wait_ge(sem["cap"], n)
                dve.scalar_tensor_tensor(em[:, :, :], cap[:, :, :], NEG_INF, l1[:, :, :], ALU.add, ALU.min)\
                    .then_inc(sem["em"], 1)
                dve.wait_ge(sem["em"], n)
                dve.tensor_reduce(nmax1[:, :], em[:, :, :], AX.X, ALU.max, negate=True).then_inc(sem["nmax1"], 1)

            def f_rden(n):
                dve.wait_ge(sem["p1"], n)
                dve.reciprocal(rden1[:, :], den1[:, :]).then_inc(sem["rden1"], 1)

            def f_x2(n):
                dve.wait_ge(sem["Hp"], n)
                dve.tensor_scalar(mn[:, :, :], f[:, 2, :].rearrange("p (g d) -> p g d", g=G), 0.0, None, ALU.min)\
                    .then_inc(sem["mn"], 1)
                dve.scalar_tensor_tensor(rx[:, :, :], f[:, 2, :].rearrange("p (g d) -> p g d", g=G), 0.0, x1[:, :, :],
                                         ALU.max, ALU.add).then_inc(sem["rx"], 1)

            def f_x2_sum(n):
                dve.wait_ge(sem["rx"], n)
                dve.wait_ge(sem["ex"], n)
                dve.scalar_tensor_tensor(x2[:, :, :], ex[:, :, :], -1.0, rx[:, :, :], ALU.add, ALU.add)\
                    .then_inc(sem["x2"], 1)

            def f_h2(n):
                dve.wait_ge(sem["hn2"], n * G)
                dve.tensor_scalar(h2[:, :, :], hn[2][:, :, :], 0.0, None, ALU.max).then_inc(sem["h2"], 1)

            def f_mask(n):
                dve.wait_ge(sem["mask_in"], 16 * n)
                m = mask_u8[:, :].rearrange("a (g n) -> a g n", g=G)
                dve.tensor_copy(mrow[0:1, :, :], m)
                dve.tensor_copy(mrow0[0:1, :, :], m)
                dve.tensor_scalar(mbig[0:1, :, :], m, BIG, None, ALU.mult).then_inc(sem["mrow"], 1)

            def s_bT(n):
                dve.wait_ge(sem["MM"], n)
                dve.wait_ge(sem["bd"], n)
                dve.tensor_tensor(bT[:, :, :], bd[:, :, :], f[:, 1, 0:G * N].rearrange("p (g n) -> p g n", g=G),
                                  ALU.mult).then_inc(sem["bT"], 1)

            def s_x3(n):
                dve.wait_ge(sem["x2b"], n)
                for g in range(G):
                    dve.wait_ge(sem["OUT"], n * G - (G - 1 - g))
                    dve.tensor_tensor(x3[:, g, :], s_banks[:, g, 0:D], x2b[:, g, :], ALU.add)\
                        .then_inc(sem["x3"], 1)

            def s_k_odd(n):
                dve.wait_ge(sem["K"], n)
                dve.tensor_copy(kbd[DH:P, :, :, 1, :], s_banks[DH:P, 2:4, :].rearrange("p b (q n) -> p (b q) n", n=N))\
                    .then_inc(sem["k_odd"], 1)

            def s_max(q, n):
                dve.wait_ge(sem[f"dots{q}"], n)
                dve.tensor_reduce(half(nm, q), s_banks[:, BANKS[q], :].rearrange("p (h n) -> p h n", n=N),
                                  AX.X, ALU.max, negate=True).then_inc(sem[f"nm{q}"], 1)

            def s_rsum(q, n):
                dve.wait_ge(sem[f"pr{q}"], n)
                dve.reciprocal(half(ri, q), half(rs, q)).then_inc(sem[f"ri{q}"], 1)

            def s_at(q, n):
                dve.wait_ge(sem[f"PT{q}"], n)
                dve.tensor_tensor(half(at, q), s_banks[:, BANKS[q], :].rearrange("p (h n) -> p h n", n=N),
                                  bT[:, q // 2, :].unsqueeze(1).broadcast_to([P, HALF, N]), ALU.add).then_inc(sem[f"at{q}"], 1)

            def s_y_lo(layer, n):
                dve.wait_ge(sem[f"y{layer}"], n)
                dve.tensor_tensor(y_lo[:, :, :], y[:, :, :], y_hi[:, :, :].bitcast(fp32), ALU.subtract)\
                    .then_inc(sem[f"y{layer}_lo"], 1)

            def f_zt_lo(n):
                dve.wait_ge(sem["zt_hi"], n)
                dve.tensor_tensor(zt_lo[:, :, :].rearrange("p c n -> p (c n)"), f[:, 1, :],
                                  zt_hi[:, :, :].bitcast(fp32).rearrange("p c n -> p (c n)"), ALU.subtract)\
                    .then_inc(sem["zt_lo"], 1)

            def s_ot_lo(g, n):
                dve.wait_ge(sem[f"ot{g}_hi"], n)
                dve.tensor_tensor(ot_lo[:, g, :, :].rearrange("p h n -> p (h n)"), s_banks[:, BANKS[2 * g], :],
                                  ot_hi[:, g, :, :].bitcast(fp32).rearrange("p h n -> p (h n)"), ALU.subtract)\
                    .then_inc(sem[f"ot{g}_lo"], 1)

            def s_x4(n):
                dve.wait_ge(sem["W"], n)
                dve.wait_ge(sem["x3b"], n)
                dve.wait_ge(sem["out_done"], 16 * n)
                dve.scalar_tensor_tensor(x4[:, :, :], s_banks[:, 1, :].rearrange("p (g d) -> p g d", g=G), LA, x3b[:, :, :],
                                         ALU.mult, ALU.add).then_inc(sem["x4"], 1)

            def turn(fn, f0, f1, s, so):
                if f1 is not None:
                    dve.wait_ge(sem["x1"], f1)
                    norm_stats(1, x1, f1)
                if s is not None:
                    s_bT(s)
                if f0 is not None:
                    lo_relu(0, f[:, 0, :], h0_hi, h0_lo, f0)
                if f1 is not None:
                    norm_apply(1, x1, f1)
                if so is not None:
                    s_x4(so)
                if s is not None:
                    s_y_lo(2, s)
                if f0 is not None:
                    f_si(f0)
                    f_logits0(f0)
                if s is not None:
                    s_x3(s)
                    norm_stats(3, x3, s, sem["x3"])
                if f1 is not None:
                    lo_relu(1, s_banks[:, 2, :], h1_hi, h1_lo, f1)
                if s is not None:
                    norm_apply(3, x3, s)
                if f1 is not None:
                    f_logits1(f1)
                if s is not None:
                    lo_relu(3, s_banks[:, 2, :], h3_hi, h3_lo, s)
                if f1 is not None:
                    f_maxima1(f1)
                if f0 is not None:
                    f_transition(f0)
                if f1 is not None:
                    f_rden(f1)
                if f0 is not None:
                    f_cap(f0)
                if s is not None:
                    s_k_odd(s)
                if f1 is not None:
                    f_x2(f1)
                    f_x2_sum(f1)
                    dve.wait_ge(sem["x2"], f1)
                    norm_stats(2, x2, f1)
                if s is not None:
                    s_max(0, s)
                    s_max(1, s)
                if f1 is not None:
                    norm_apply(2, x2, f1)
                if s is not None:
                    s_rsum(0, s)
                if f1 is not None:
                    f_h2(f1)
                if s is not None:
                    s_max(2, s)
                    s_rsum(1, s)
                    s_max(3, s)
                    s_at(0, s)
                    s_rsum(2, s)
                    s_at(1, s)
                    s_rsum(3, s)
                if f1 is not None:
                    f_zt_lo(f1)
                if s is not None:
                    s_at(2, s)
                    s_ot_lo(0, s)
                    s_at(3, s)
                if fn is not None:
                    f_norm0(fn)
                if f1 is not None:
                    f_mask(f1)
                if fn is not None:
                    norm_apply(0, x0, fn)
                if f1 is not None:
                    s_y_lo(1, f1)
                if s is not None:
                    s_ot_lo(1, s)
                if f0 is not None:
                    f_x1(f0)

            turn(1, None, None, None, None)
            turn(2, 1, None, None, None)
            turn(3, 2, 1, None, None)
            turn(4, 3, 2, 1, None)
            with dve.Fori(2, PAIRS - 2) as t:
                turn(t + 3, t + 2, t + 1, t, t - 1)
            turn(None, PAIRS, PAIRS - 1, PAIRS - 2, PAIRS - 3)
            turn(None, None, PAIRS, PAIRS - 1, PAIRS - 2)
            turn(None, None, None, PAIRS, PAIRS - 1)
            turn(None, None, None, None, PAIRS)

        @block.tensor
        def _(pe):
            def mm(o, lhsT, rhs, start=True, stop=True, **kw):
                return pe.matmul(o, lhsT, rhs, start=start, stop=stop, **kw)

            def chunks3(o, pairs, start=True, stop=True, **kw):
                for i, (lh, ll, rh, rl) in enumerate(pairs):
                    mm(o, ll, rh, start=start and i == 0, stop=False, **kw)
                    mm(o, lh, rl, start=False, stop=False, **kw)
                    last = mm(o, lh, rh, start=False, stop=stop and i == len(pairs) - 1, **kw)
                return last

            def transposes(bank, k, n):
                for g in range(G):
                    pe.wait_ge(sem[f"hn{k}"], n * G - (G - 1 - g))
                    for c in range(C):
                        o = (c * G + g) * N
                        tile = hn[k]
                        last = pe.transpose(bank[:, o:o + N], tile[:, g, c * P:(c + 1) * P], ident[:, :])
                return last

            def hi_first(banks, by_chunk=None):
                for c in range(C):
                    if by_chunk is not None:
                        by_chunk(c)
                    for bank in banks:
                        for r, (o, early, _) in enumerate(bank):
                            for i in range(2):
                                mm(o, *early[c * 2 + i], start=(c == 0 and r == 0 and i == 0), stop=False,
                                   skip_group_check=True)

            def lo_last(banks):
                for bank in banks:
                    for o, _, late in bank:
                        for a, b in late:
                            last = mm(o, a, b, start=False, skip_group_check=True)
                return last

            def as_moving(o, w_hi, w_lo, h_hi, h_lo):
                early = [(w(c), h_hi[:, c, :, :]) for c in range(C) for w in (w_lo, w_hi)]
                return o, early, [(w_hi(c), h_lo[:, c, :, :]) for c in range(C)]

            def as_stationary(o, g, h_hi, h_lo, w_hi, w_lo):
                early = [(h_hi[:, c, g, :], w(c)) for c in range(C) for w in (w_lo, w_hi)]
                return o, early, [(h_lo[:, c, g, :], w_hi(c)) for c in range(C)]

            def by_node(hi, lo, g, w_hi, w_lo):
                return [(hi[:, c, g, :], lo[:, c, g, :], w_hi(c), w_lo(c)) for c in range(C)]

            def f_transpose_h(n, f1):
                if f1 is not None:
                    pe.wait_ge(sem["s1"], f1)
                transposes(f[:, 0, :], 0, n).then_inc(sem["T_h0"], 1)

            def f_transpose_adj(n, f1):
                pe.wait_ge(sem["adj_in"], 16 * n)
                if f1 is not None:
                    pe.wait_ge(sem["z1"], f1)
                for g in range(G):
                    last = pe.transpose(f[:, 1, g * N:(g + 1) * N], adj_ij[:, g, :], ident[:, :])
                last.then_inc(sem["T_adj"], 1)

            def f_logits0(n):
                pe.wait_ge(sem["h0_lo"], n)
                chunks3(s_banks[:, 3, 0:G * N], [(v0_hi[:, c, :], v0_lo[:, c, :], h0_hi[:, c, :, :], h0_lo[:, c, :, :])
                                           for c in range(C)]).then_inc(sem["E0"], 1)

            def f_hop2(n, f1):
                pe.wait_ge(sem["h0_lo"], n)
                if f1 is not None:
                    pe.wait_ge(sem["xt"], f1)
                for g in range(G):
                    last = chunks3(f[:, 2 + g, 0:EXT], by_node(h0_hi, h0_lo, g, lambda c: k_hi[:, c, 2, :],
                                                               lambda c: k_lo[:, c, 2, :]))
                last.then_inc(sem["S2p"], 1)

            def f_hop1(n, f1):
                pe.wait_ge(sem["h0_lo"], n)
                for g in range(G):
                    chunks3(f[:, 0, g * D:(g + 1) * D], by_node(h0_hi, h0_lo, g, lambda c: k_hi[:, c, 1, 0:D],
                                                                lambda c: k_lo[:, c, 1, 0:D]),
                            start=(g == 0), stop=False, skip_group_check=True)

            def f_trT(n):
                pe.wait_ge(sem["tr"], n)
                pe.wait_ge(sem["adjT"], n)
                for g in range(G):
                    last = pe.transpose(f[:, 1, g * N:(g + 1) * N], tr[:, g, :], ident[:, :])
                last.then_inc(sem["TT"], 1)

            def f_aggregate(bank, src, made, done, n):
                pe.wait_ge(sem["trT"], n)
                pe.wait_ge(sem[made], n)
                for g in range(G):
                    last = mm(f[:, bank, g * D:(g + 1) * D], trT[:, g, :], src[:, g, 0:D], start=False,
                              skip_group_check=True)
                last.then_inc(sem[done], 1)

            def f_hop0(n, s):
                if s is not None:
                    pe.wait_ge(sem["rx"], s)
                for g in range(G):
                    chunks3(f[:, 2, g * D:(g + 1) * D], by_node(h0_hi, h0_lo, g, lambda c: k_hi[:, c, 0, 0:D],
                                                                lambda c: k_lo[:, c, 0, 0:D]),
                            start=(g == 0), stop=False, skip_group_check=True)

            def f_transpose1(n, f0):
                transposes(s_banks[:, 2, :], 1, n).then_inc(sem["T_h1"], 1)

            def f_products1(n, f0, s):
                pe.wait_ge(sem["h1_hi"], n)
                logits = [[as_moving(f[:, 1, 0:G * N], lambda c: v1_hi[:, c, :], lambda c: v1_lo[:, c, :], h1_hi, h1_lo)]]
                wh = [[as_stationary(f[:, 2 + g, 0:EXT], g, h1_hi, h1_lo, lambda c: w1_hi[:, c, :], lambda c: w1_lo[:, c, :])]
                      for g in range(G)]
                if s is not None:
                    pe.wait_ge(sem["bT"], s)
                hi_first(logits)
                if f0 is not None:
                    pe.wait_ge(sem["s2"], f0)
                hi_first(wh)
                pe.wait_ge(sem["h1_lo"], n)
                lo_last(logits)
                lo_last(wh).then_inc(sem["Wh"], 1)

            def f_attend1(n):
                pe.wait_ge(sem["whs"], n)
                for g in range(G):
                    last = mm(f[:, 2, g * D:(g + 1) * D], p1[:, g, :], whs[:, g, :])
                last.then_inc(sem["Hp"], 1)

            def f_aggregate_h(n, s):
                pe.wait_ge(sem["h2"], n)
                pe.wait_ge(sem["adjs"], n)
                for c in range(C):
                    for g in range(G):
                        o = (c * G + g) * N
                        last = mm(f[:, 1, o:o + N], h2[:, g, c * P:(c + 1) * P], adjs[:, g, :])
                last.then_inc(sem["ZT"], 1)

            def s_mask(n):
                pe.wait_ge(sem["mrow"], n)
                for g in range(G):
                    last = mm(f[:, 1, g * N:(g + 1) * N], mrow0[:, g, :], mrow0[:, g, :])
                last.then_inc(sem["MM"], 1)

            def s_first(n):
                pe.wait_ge(sem["zt_lo"], n)
                for o in range(C):
                    cols = slice(o * P, (o + 1) * P)
                    last = chunks3(f[:, 3, o * G * N:(o + 1) * G * N],
                                   [(g1_hi[:, c, cols], g1_lo[:, c, cols], zt_hi[:, c, :], zt_lo[:, c, :]) for c in range(C)])
                last.then_inc(sem["Y1"], 1)

            def s_support(bank, w_hi, w_lo):
                return [[as_stationary(s_banks[:, bank, g * D:(g + 1) * D], g, y_hi[:, :, :].rearrange("p c (g n) -> p c g n", g=G),
                                       y_lo[:, :, :].rearrange("p c (g n) -> p c g n", g=G),
                                       lambda c: w_hi[:, c, :], lambda c: w_lo[:, c, :]) for g in range(G)]]

            def s_support_a(n):
                a = s_support(2, g2_hi, g2_lo)
                pe.wait_ge(sem["y1_lo"], n)
                hi_first(a)
                lo_last(a).then_inc(sem["SA"], 1)

            def s_support_b(n):
                pe.wait_ge(sem["y2_hi"], n)
                pe.wait_ge(sem["x4"], n)
                b = s_support(1, g3_hi, g3_lo)
                hi_first(b)
                pe.wait_ge(sem["y2_lo"], n)
                lo_last(b).then_inc(sem["SB"], 1)

            def s_second(n):
                pe.wait_ge(sem["supa"], n)
                for o in range(C):
                    for g in range(G):
                        at_ = (o * G + g) * N
                        last = mm(s_banks[:, 3, at_:at_ + N], sup[:, g, o * P:(o + 1) * P], adjs[:, g, :])
                last.then_inc(sem["Y2"], 1)

            def s_third(n):
                pe.wait_ge(sem["supb"], n)
                for g in range(G):
                    mm(s_banks[:, g, 0:D], adjs[:, g, :], sup[:, g, :]).then_inc(sem["OUT"], 1)

            def s_transpose3(n):
                transposes(s_banks[:, 2, :], 3, n).then_inc(sem["T_h3"], 1)

            def s_heads(kind, bank, n):
                def region(hp):
                    a = kind * INNER + hp * P
                    return as_moving(s_banks[:, bank + hp // 2, (hp % 2) * G * N:(hp % 2 + 1) * G * N],
                                     lambda c: qkv_hi[:, c, a:a + P], lambda c: qkv_lo[:, c, a:a + P], h3_hi, h3_lo)
                return [[region(hp) for hp in range(b * HP // 2, (b + 1) * HP // 2)] for b in range(2)]

            def s_queries(n):
                q = s_heads(0, 0, n)
                hi_first(q, lambda c: pe.wait_ge(sem["h3_hi"], n * C - (C - 1 - c)))
                pe.wait_ge(sem["h3_lo"], n)
                lo_last(q).then_inc(sem["Q"], 1)

            def s_keys(n, f0):
                if f0 is not None:
                    pe.wait_ge(sem["z0"], f0)
                k = s_heads(1, 2, n)
                hi_first(k)
                lo_last(k).then_inc(sem["K"], 1)

            def s_values(n):
                pe.wait_ge(sem["q"], n)
                a = 2 * INNER
                for g in range(G):
                    last = chunks3(s_banks[:, g, :], by_node(h3_hi, h3_lo, g, lambda c: qkv_hi[:, c, a:a + INNER],
                                                       lambda c: qkv_lo[:, c, a:a + INNER]))
                last.then_inc(sem["V"], 1)

            def s_dots(q, n):
                if q == 0:
                    pe.wait_ge(sem["k_even"], n)
                    pe.wait_ge(sem["k_odd"], n)
                if q == 2:
                    pe.wait_ge(sem["v"], n)
                g, bank = q // 2, s_banks[:, BANKS[q], :]
                mm(bank, mrow[:, g, :], mbig[:, g, :].unsqueeze(1).broadcast_to([P, HALF, N]), stop=False,
                   skip_group_check=True)
                for i in range(2):
                    hp = 2 * (q % 2) + i
                    last = mm(bank[:, i * 2 * N:(i + 1) * 2 * N], qT[:, hp, g, :], kbd[:, hp, g, :, :], start=False,
                              skip_group_check=True)
                last.then_inc(sem[f"dots{q}"], 1)

            def s_transpose_p(q, n):
                pe.wait_ge(sem[f"pn{q}"], n)
                for i in range(HALF):
                    last = pe.transpose(s_banks[:, BANKS[q], i * N:(i + 1) * N], half(pn, q)[:, i, :], ident[:, :])
                last.then_inc(sem[f"PT{q}"], 1)

            def s_attend(q, n):
                g = q // 2
                pe.wait_ge(sem[f"at{q}"], n)
                for i in range(HALF):
                    h = HALF * (q % 2) + i
                    rows, hp = (h % 2) * DH, h // 2
                    last = mm(s_banks[rows:rows + DH, BANKS[2 * g], hp * N:(hp + 1) * N], v[:, g, h * DH:(h + 1) * DH],
                              at[:, g, h, :])
                if q % 2 == 1:
                    last.then_inc(sem[f"PV{g}"], 1)

            def s_project(g, n):
                pe.wait_ge(sem[f"ot{g}_lo"], n)
                if g == 0:
                    pe.wait_ge(sem["at3"], n)
                last = chunks3(s_banks[:, 1, g * D:(g + 1) * D], [(ot_hi[:, g, hp, :], ot_lo[:, g, hp, :],
                                                                   wout_hi[:, hp, :], wout_lo[:, hp, :]) for hp in range(HP)])
                if g == G - 1:
                    last.then_inc(sem["W"], 1)

            def turn(f0, f1, s, so):
                if s is not None:
                    s_support_a(s)
                if f0 is not None:
                    f_transpose_h(f0, f1)
                if so is not None:
                    s_project(1, so)
                if s is not None:
                    s_second(s)
                if f0 is not None:
                    f_hop2(f0, f1)
                if s is not None:
                    s_support_b(s)
                if f0 is not None:
                    f_logits0(f0)
                if f1 is not None:
                    f_transpose1(f1, f0)
                if s is not None:
                    s_third(s)
                if f0 is not None:
                    f_hop1(f0, f1)
                if f1 is not None:
                    f_products1(f1, f0, s)
                if s is not None:
                    s_transpose3(s)
                if f0 is not None:
                    f_transpose_adj(f0, f1)
                if s is not None:
                    s_queries(s)
                    s_keys(s, f0)
                if f1 is not None:
                    f_attend1(f1)
                if s is not None:
                    s_values(s)
                if f0 is not None:
                    f_trT(f0)
                if s is not None:
                    for q in range(4):
                        s_dots(q, s)
                if f0 is not None:
                    f_aggregate(0, s2, "s2", "A0", f0)
                if s is not None:
                    s_transpose_p(0, s)
                if f1 is not None:
                    f_aggregate_h(f1, s)
                if s is not None:
                    s_transpose_p(1, s)
                    s_attend(0, s)
                if f0 is not None:
                    f_hop0(f0, f1)
                if s is not None:
                    s_transpose_p(2, s)
                    s_attend(1, s)
                    s_transpose_p(3, s)
                if f1 is not None:
                    s_first(f1)
                if s is not None:
                    s_attend(2, s)
                    s_project(0, s)
                    s_attend(3, s)
                if f1 is not None:
                    s_mask(f1)
                if f0 is not None:
                    f_aggregate(2, s1, "s1", "B0", f0)

            pe.wait_ge(sem["id_set"], 1)
            pe.wait_ge(sem["w_split"], 1)
            pe.wait_ge(sem["pad2_set"], 1)
            turn(1, None, None, None)
            pe.wait_ge(sem["w_g1"], 1)
            turn(2, 1, None, None)
            pe.wait_ge(sem["pad_set"], 1)
            pe.wait_ge(sem["w_ready"], 1)
            turn(3, 2, 1, None)
            with pe.Fori(2, PAIRS - 1) as t:
                turn(t + 2, t + 1, t, t - 1)
            turn(None, PAIRS, PAIRS - 1, PAIRS - 2)
            turn(None, None, PAIRS, PAIRS - 1)
            turn(None, None, None, PAIRS)


_INS = ["x", "adj", "nodemask", "L0_gnn_Wv", "L0_gnn_bv", "L0_gnn_aw", "L0_gnn_ab", "L0_gnn_Wk", "L0_gnn_bk",
        "L1_gnn_W", "L1_gnn_a", "L2_gnn_W1", "L2_gnn_b1", "L2_gnn_W2", "L2_gnn_b2", "L2_gnn_W3", "L2_gnn_b3",
        "L3_gnn_W_qkv", "L3_gnn_W_out", "L3_gnn_b_out"]


def kernel(**inputs):
    import numpy as _np
    import concourse.bacc as _bacc
    from concourse import mybir as _mybir
    from concourse.bass_utils import run_bass_kernel_spmd as _run

    nc = _bacc.Bacc("TRN2", target_bir_lowering=False, num_devices=1)
    arrays, args = {}, []
    for name in _INS:
        a = _np.ascontiguousarray(inputs[name])
        if a.dtype == bool:
            a = a.view(_np.uint8)
        arrays[f"in_{name}"] = a
        args.append(nc.dram_tensor(f"in_{name}", a.shape, _mybir.dt.from_np(a.dtype), kind="ExternalInput").ap())
    shape = inputs["x"].shape
    args.append(nc.dram_tensor("out_x", shape, _mybir.dt.float32, kind="ExternalOutput").ap())
    build(nc, *args)
    r = _run(nc, [arrays], core_ids=[0])
    return r.results[0]["out_x"]
```

```python
import concourse.bass as bass
from concourse import mybir
from contextlib import ExitStack


def build(nc, x, adj, nodemask, l0_wv, l0_bv, l0_aw, l0_ab, l0_wk, l0_bk, l1_w, l1_a,
          l2_w1, l2_b1, l2_w2, l2_b2, l2_w3, l2_b3, l3_wqkv, l3_wout, l3_bout, out):
    fp32 = mybir.dt.float32
    f32r = mybir.dt.float32r
    bf16 = mybir.dt.bfloat16
    ALU = mybir.AluOpType
    ACT = mybir.ActivationFunctionType
    AX = mybir.AxisListType

    GRAPHS, N, D = x.shape
    P = 128
    C = D // P
    G = 2
    PAIRS = GRAPHS // G
    HEADS = 8
    DH = l3_wout.shape[0] // HEADS
    INNER = HEADS * DH
    HP = HEADS // 2
    KHOPS = l0_wk.shape[0]
    EXT = D + 2
    EPS = 1e-5
    ROW_EPS = 1e-12
    SLOPE = 0.2
    NEG_INF = -9e15
    CAP = 3e38
    BIG = 2.0 ** 127
    SCALE = float(DH) ** -0.5
    LA = 0.33

    ctx = ExitStack()
    with ctx:
        def sb(name, shape, dt=fp32):
            return ctx.enter_context(nc.sbuf_tensor(name, shape, dt))

        ident = sb("ident", [P, P])
        pr_area = sb("pr_area", [P, 3 * C * INNER])
        w_raw = pr_area[:, :].rearrange("p (c n) -> p c n", c=C)
        x4_area = sb("x4_area", [P, C * D])
        wv_raw = x4_area[:, :].rearrange("p (c n) -> p c n", c=C)
        mn = sb("mn", [P, G, D])
        ex = sb("ex", [P, G, D])
        aw_bc, a_bc = mn, ex
        v_area = sb("v_area", [P, G * INNER])
        bv_bc = v_area[:, KHOPS * D:(KHOPS + 1) * D]
        bk_bc = v_area[:, 0:KHOPS * D].rearrange("p (k n) -> p k n", k=KHOPS)
        ab_bc = sb("ab_bc", [P, 1])
        at_area = sb("at_area", [P, 10 * D])
        products = at_area[:, :].rearrange("p (k n) -> p k n", k=10)
        att0 = sb("att0", [P, C, 2])
        att1 = sb("att1", [P, C, 2])
        c_part = sb("c_part", [P, 3])
        c0 = sb("c0", [P, 1])
        k_hi = sb("k_hi", [P, C, KHOPS, EXT], f32r)
        k_lo = sb("k_lo", [P, C, KHOPS, EXT], f32r)
        w1_hi = sb("w1_hi", [P, C, EXT], f32r)
        w1_lo = sb("w1_lo", [P, C, EXT], f32r)
        gb1 = sb("gb1", [P, C])
        gb2 = sb("gb2", [P, C])
        b3_bc = sb("b3_bc", [P, D])
        qkv_hi = sb("qkv_hi", [P, C, 3 * INNER], f32r)
        qkv_lo = sb("qkv_lo", [P, C, 3 * INNER], f32r)
        pn_area = sb("pn_area", [P, G * HEADS * N])
        wout = pn_area[:, 0:HP * D].rearrange("p (h n) -> p h n", h=HP)
        g1 = pn_area[:, HP * D:(HP + C) * D].rearrange("p (c n) -> p c n", c=C)
        wout_hi = sb("wout_hi", [P, HP, D], f32r)
        wout_lo = sb("wout_lo", [P, HP, D], f32r)
        g2 = pn_area[:, (HP + C) * D:(HP + 2 * C) * D].rearrange("p (c n) -> p c n", c=C)
        x2b = sb("x2b", [P, G, D])
        g3 = x2b
        g2_hi = sb("g2_hi", [P, C, D], f32r)
        g2_lo = sb("g2_lo", [P, C, D], f32r)
        g3_hi = sb("g3_hi", [P, C, D], f32r)
        g3_lo = sb("g3_lo", [P, C, D], f32r)
        g1_hi = sb("g1_hi", [P, C, D], f32r)
        g1_lo = sb("g1_lo", [P, C, D], f32r)
        bout_bc = sb("bout_bc", [P, D])
        bsum = sb("bsum", [P, D])
        bsum_a = sb("bsum_a", [P, D])
        spare = sb("spare", [P, 1])
        zero = sb("zero", [P, 1])
        expo = sb("expo", [P, G])

        x0 = sb("x0", [P, G, D])
        xr = sb("xr", [P, G, D])
        adj_ij = sb("adj_ij", [P, G, N])
        mask_u8 = sb("mask_u8", [1, G * N], mybir.dt.uint8)
        stats = [sb(f"stats{k}", [P, G, 6]) for k in range(4)]
        mv = [sb(f"mv{k}", [P, G, 2]) for k in range(4)]
        veps = [sb(f"veps{k}", [P, G]) for k in range(4)]
        rstd = [sb(f"rstd{k}", [P, G]) for k in range(4)]
        hn = [sb(f"hn{k}", [P, G, D]) for k in range(4)]
        h2 = sb("h2", [P, G, D])
        h0_hi = sb("h0_hi", [P, C, G, N], f32r)
        h0_lo = sb("h0_lo", [P, C, G, N], f32r)
        h1_hi = sb("h1_hi", [P, C, G, N], f32r)
        h1_lo = sb("h1_lo", [P, C, G, N], f32r)
        h3_hi = sb("h3_hi", [P, C, G, N], f32r)
        h3_lo = sb("h3_lo", [P, C, G, N], f32r)
        adj_ji = sb("adj_ji", [P, G, N])
        adjs = sb("adjs", [P, G, N])
        sic = sb("sic", [P, G])
        z0 = sb("z0", [P, G, N])
        l0 = sb("l0", [P, G, N])
        e0 = sb("e0", [P, G, N])
        alpha = sb("alpha", [P, G, N])
        rsum = sb("rsum", [P, G])
        rsume = sb("rsume", [P, G])
        rinv = sb("rinv", [P, G])
        tr = sb("tr", [P, G, N])
        trT = sb("trT", [P, G, N])
        s2 = sb("s2", [P, G, EXT])
        s1 = sb("s1", [P, G, D])
        xt = sb("xt", [P, G, D])
        x1 = sb("x1", [P, G, D])
        cap = sb("cap", [P, G, N])
        wh2 = sb("wh2", [P, G, 2])
        z1 = sb("z1", [P, G, N])
        l1 = sb("l1", [P, G, N])
        em = sb("em", [P, G, N])
        nmax1 = sb("nmax1", [P, G])
        p1 = sb("p1", [P, G, N])
        den1 = sb("den1", [P, G])
        rden1 = sb("rden1", [P, G])
        whs = sb("whs", [P, G, D])
        rx = sb("rx", [P, G, D])
        x2 = sb("x2", [P, G, D])
        zt_hi = sb("zt_hi", [P, C, G * N], f32r)
        zt_lo = sb("zt_lo", [P, C, G * N], f32r)
        y = sb("y", [P, C, G * N])
        y_hi = sb("y_hi", [P, C, G * N], f32r)
        y_lo = sb("y_lo", [P, C, G * N], f32r)
        sup = sb("sup", [P, G, D])
        x3 = sb("x3", [P, G, D])
        x3b = sb("x3b", [P, G, D])
        mrow = sb("mrow", [P, G, N], bf16)
        mrow0 = sb("mrow0", [P, G, N], bf16)
        mbig = sb("mbig", [P, G, N], bf16)
        ed = sb("ed", [P, G, N])
        bd = sb("bd", [P, G, N])
        bT = sb("bT", [P, G, N])
        qT = sb("qT", [P, HP, G, N])
        kbd = sb("kbd", [P, HP, G, 2, N])
        v = v_area[:, :].rearrange("p (g n) -> p g n", g=G)
        nm = sb("nm", [P, G, HEADS])
        rs = sb("rs", [P, G, HEADS])
        ri = sb("ri", [P, G, HEADS])
        pr = pr_area[:, 0:G * HEADS * N].rearrange("p (g h n) -> p g h n", g=G, h=HEADS)
        pn = pn_area[:, :].rearrange("p (g h n) -> p g h n", g=G, h=HEADS)
        at = at_area[:, 0:G * HEADS * N].rearrange("p (g h n) -> p g h n", g=G, h=HEADS)
        ot_hi = sb("ot_hi", [P, G, HP, N], f32r)
        ot_lo = sb("ot_lo", [P, G, HP, N], f32r)
        x4 = x4_area[:, :].rearrange("p (g n) -> p g n", g=G)

        f = ctx.enter_context(nc.psum_tensor("f", [P, 4, 512], fp32))
        s_banks = ctx.enter_context(nc.psum_tensor("s_banks", [P, 4, 512], fp32))

        HALF = HEADS // 2
        BANKS = (2, 3, 0, 1)

        def half(tile, q):
            return tile[:, q // 2, HALF * (q % 2):HALF * (q % 2 + 1)]

        names = """
            w_in w_in2 w_in3 w_hi w_att w_c w_bsum w_split w_split3 pad_set id_zero id_set
            mask_pad expo_set x_in adj_in mask_in out_done T_h0 T_adj xr adjT h0_hi h0_lo E0 S2p si z0 l0 e0
            alpha rsume rinv tr TT trT s2 A0 s1 B0 xt x1 T_h1 h1_hi h1_lo Wh cap E1 wh2 z1 l1 em nmax1 p1 rden1 whs
            Hp mn ex rx x2 h2 adjs x2b ZT MM zt_hi zt_lo Y1 y1_hi y1 y1_lo SA supa Y2 y2_hi y2 y2_lo SB supb OUT
            x3 x3b ed bd bT T_h3 h3_hi h3_lo Q q K k_even k_odd V v mrow PV0 PV1 ot0_hi ot1_hi ot0_lo ot1_lo
            W0 W1 x4_0 x4_1 w_split2""".split()
        sem = {n: ctx.enter_context(nc.semaphore(n)) for n in names}
        for k in range(4):
            for n in ("stats", "mv", "veps", "rstd", "hn", "dots", "nm", "pr", "ri", "pn", "PT", "at"):
                sem[f"{n}{k}"] = ctx.enter_context(nc.semaphore(f"{n}_{k}"))

        block = ctx.enter_context(nc.Block())

        def pair_rows(a, t):
            if isinstance(t, int):
                return a[t * G:(t + 1) * G].rearrange("g n d -> n g d")
            return a[bass.ds(t * G, G)].rearrange("g n d -> n g d")

        def pair_mask(start):
            m = nodemask.rearrange("(a g) n -> a (g n)", a=1)
            return m[:, start:start + G * N] if isinstance(start, int) else m[:, bass.ds(start, G * N)]

        def per_graph(b):
            return b[:, :].unsqueeze(1).broadcast_to([P, G, D])

        LOADS1 = 8 + 2 * KHOPS
        LOADS2 = 3 * C
        LOADS3 = 8

        @block.sync
        def _(sp):
            def row_bc(a, width):
                return a.rearrange("(a n) -> a n", a=1).broadcast_to([P, width])

            def load_mask(start):
                sp.dma_start(mask_u8[:, :], pair_mask(start)).then_inc(sem["mask_in"], 16)

            sp.dma_start(x0[:, :, :], pair_rows(x, 0)).then_inc(sem["x_in"], 16)
            sp.dma_start(adj_ij[:, :, :], pair_rows(adj, 0)).then_inc(sem["adj_in"], 16)
            load_mask(0)
            n1 = [sp.dma_start(wv_raw[:, :, :], l0_wv.rearrange("(c p) n -> p c n", c=C)),
                  sp.dma_start(w_raw[:, :, 3 * D:4 * D], l1_w.rearrange("(c p) n -> p c n", c=C)),
                  sp.dma_start(bv_bc[:, :], row_bc(l0_bv, D)),
                  sp.dma_start(ab_bc[:, :], row_bc(l0_ab, 1))]
            for j in range(2):
                n1.append(sp.dma_start(aw_bc[:, j, :], row_bc(l0_aw[j * D:(j + 1) * D, :].rearrange("n a -> (n a)"), D)))
                n1.append(sp.dma_start(a_bc[:, j, :], row_bc(l1_a[j * D:(j + 1) * D, :].rearrange("n a -> (n a)"), D)))
            for k in range(KHOPS):
                n1.append(sp.dma_start(w_raw[:, :, k * D:(k + 1) * D], l0_wk[k].rearrange("(c p) n -> p c n", c=C)))
                n1.append(sp.dma_start(bk_bc[:, k, :], row_bc(l0_bk[k], D)))
            for d in n1:
                d.then_inc(sem["w_in"], 16)
            assert len(n1) == LOADS1
            n3 = [sp.dma_start(g[:, :, :], w.rearrange("(c p) n -> p c n", c=C))
                  for g, w in ((g1, l2_w1), (g2, l2_w2), (g3, l2_w3))]
            n3 += [sp.dma_start(g[:, :], b.rearrange("(c p) -> p c", c=C), allow_slow_non_contiguous=True) 
                   for g, b in ((gb1, l2_b1), (gb2, l2_b2))]
            n3 += [sp.dma_start(b3_bc[:, :], row_bc(l2_b3, D)), sp.dma_start(bout_bc[:, :], row_bc(l3_bout, D)),
                   sp.dma_start(wout[:, :, :], l3_wout.rearrange("(c p) n -> p c n", c=HP))]
            assert len(n3) == LOADS3
            for d in n3:
                d.then_inc(sem["w_in3"], 16)
            sp.wait_ge(sem["w_split"], 1)
            for c in range(C):
                for kind in range(3):
                    src = l3_wqkv[c * P:(c + 1) * P, :].rearrange("p (h k d) -> p h k d", h=HEADS, k=3)[:, :, kind, :]
                    dst = w_raw[:, c, kind * INNER:(kind + 1) * INNER].rearrange("p (h d) -> p h d", h=HEADS)
                    sp.dma_start(dst, src).then_inc(sem["w_in2"], 16)

            def load_adj(t, n):
                sp.wait_ge(sem["tr"], n)
                sp.wait_ge(sem["T_adj"], n)
                sp.dma_start(adj_ij[:, :, :], pair_rows(adj, t)).then_inc(sem["adj_in"], 16)

            def load_x(t, n):
                sp.wait_ge(sem["xr"], n)
                sp.wait_ge(sem["T_h0"], n)
                sp.dma_start(x0[:, :, :], pair_rows(x, t)).then_inc(sem["x_in"], 16)

            def store(t, n):
                sp.wait_ge(sem["x4_1"], n)
                sp.dma_start(pair_rows(out, t), x4[:, :, :]).then_inc(sem["out_done"], 16)

            load_x(1, 1)
            load_adj(1, 1)
            sp.sem_inc(sem["out_done"], 16)
            load_x(2, 2)
            load_adj(2, 2)
            sp.wait_ge(sem["mrow"], 1)
            load_mask(G * N)
            with sp.Fori(1, PAIRS - 2) as t:
                load_x(t + 2, t + 2)
                load_adj(t + 2, t + 2)
                sp.wait_ge(sem["mrow"], t + 1)
                load_mask(t * (G * N) + G * N)
                store(t - 1, t)
            sp.wait_ge(sem["mrow"], PAIRS - 1)
            load_mask((PAIRS - 1) * G * N)
            store(PAIRS - 3, PAIRS - 2)
            store(PAIRS - 2, PAIRS - 1)
            store(PAIRS - 1, PAIRS)
            sp.wait_ge(sem["out_done"], 16 * (PAIRS + 1))

        @block.gpsimd
        def _(gp):
            gp.memset(zero[:, :], 0.0)
            gp.memset(expo[:, :], -0.5).then_inc(sem["expo_set"], 1)
            gp.memset(ident[:, :], 0.0).then_inc(sem["id_zero"], 1)
            gp.wait_ge(sem["id_zero"], 1)
            gp.affine_select(out=ident[:, :], in_=ident[:, :], compare_op=ALU.not_equal, fill=1.0,
                             base=0, pattern=[[-1, P]], channel_multiplier=1).then_inc(sem["id_set"], 1)
            gp.memset(kbd[:, :, :, :, :], 0.0).then_inc(sem["pad_set"], 1)
            gp.wait_ge(sem["expo_set"], 1)

            def power(k, n):
                gp.wait_ge(sem[f"veps{k}"], n)
                gp.tensor_tensor(rstd[k][:, :], veps[k][:, :], expo[:, :], ALU.pow).then_inc(sem[f"rstd{k}"], 1)

            def distance(n):
                gp.wait_ge(sem["ed"], n)
                gp.tensor_tensor(bd[:, :, :], adjs[:, :, :], ed[:, :, :], ALU.add).then_inc(sem["bd"], 1)

            def x3_bias(n, so):
                gp.wait_ge(sem["x3"], n * G)
                if so is not None:
                    gp.wait_ge(sem["x4_1"], so)
                gp.tensor_tensor(x3b[:, :, :], x3[:, :, :], per_graph(bout_bc), ALU.add).then_inc(sem["x3b"], 1)

            def probs(q, n):
                gp.wait_ge(sem[f"ri{q}"], n)
                gp.tensor_tensor(half(pn, q), half(pr, q), half(ri, q).unsqueeze(2).broadcast_to([P, HALF, N]), ALU.mult)\
                    .then_inc(sem[f"pn{q}"], 1)

            def copy_adj(f1, s):
                if s is not None:
                    gp.wait_ge(sem["bT"], s)
                    gp.wait_ge(sem["OUT"], s * G)
                gp.wait_ge(sem["adjT"], f1)
                gp.tensor_tensor(adjs[:, :, :], adj_ji[:, :, :], zero[:, :].unsqueeze(2).broadcast_to([P, G, N]), ALU.add)\
                    .then_inc(sem["adjs"], 1)

            def x2_bias(f1, s):
                if s is not None:
                    gp.wait_ge(sem["x3"], s * G)
                gp.wait_ge(sem["x2"], f1)
                gp.tensor_tensor(x2b[:, :, :], x2[:, :, :], per_graph(b3_bc), ALU.add).then_inc(sem["x2b"], 1)

            def turn(fn, f1, s, so):
                if f1 is not None:
                    power(1, f1)
                    copy_adj(f1, s)
                if s is not None:
                    power(3, s)
                if f1 is not None:
                    distance(f1)
                if s is not None:
                    x3_bias(s, so)
                if f1 is not None:
                    power(2, f1)
                if s is not None:
                    for q in range(4):
                        probs(q, s)
                if f1 is not None:
                    x2_bias(f1, s)
                if fn is not None:
                    power(0, fn)

            turn(1, None, None, None)
            turn(2, None, None, None)
            gp.wait_ge(sem["w_in3"], 16 * LOADS3)
            turn(3, 1, None, None)
            turn(4, 2, 1, None)
            with gp.Fori(2, PAIRS - 2) as t:
                turn(t + 3, t + 1, t, t - 1)
            turn(None, PAIRS - 1, PAIRS - 2, PAIRS - 3)
            turn(None, PAIRS, PAIRS - 1, PAIRS - 2)
            turn(None, None, PAIRS, PAIRS - 1)

        @block.scalar
        def _(act):
            def copy(o, i):
                return act.activation(o, i, ACT.Copy)

            def f_x_copy(n, f1):
                act.wait_ge(sem["x_in"], 16 * n)
                if f1 is not None:
                    act.wait_ge(sem["x1"], f1)
                copy(xr[:, :, :], x0[:, :, :]).then_inc(sem["xr"], 1)

            def f_h0(n):
                act.wait_ge(sem["T_h0"], n)
                act.activation(h0_hi[:, :, :, :], f[:, 0, :], ACT.Relu).then_inc(sem["h0_hi"], 1)

            def f_adj(n, f1):
                act.wait_ge(sem["T_adj"], n)
                if f1 is not None:
                    act.wait_ge(sem["cap"], f1)
                    act.wait_ge(sem["adjs"], f1)
                copy(adj_ji[:, :, :], f[:, 1, 0:G * N]).then_inc(sem["adjT"], 1)

            def f_s2(n):
                act.wait_ge(sem["S2p"], n)
                copy(s2[:, :, :], f[:, 2:4, 0:EXT]).then_inc(sem["s2"], 1)

            def f_exp0(n):
                act.wait_ge(sem["l0"], n)
                act.activation(e0[:, :, :], l0[:, :, :], ACT.Exp).then_inc(sem["e0"], 1)

            def f_trT(n):
                act.wait_ge(sem["TT"], n)
                copy(trT[:, :, :], f[:, 1, 0:G * N]).then_inc(sem["trT"], 1)

            def f_s1(n):
                act.wait_ge(sem["A0"], n)
                copy(s1[:, :, :], f[:, 0, :]).then_inc(sem["s1"], 1)

            def f_h1(n):
                act.wait_ge(sem["T_h1"], n)
                act.activation(h1_hi[:, :, :, :], s_banks[:, 2, :], ACT.Relu).then_inc(sem["h1_hi"], 1)

            def f_att1(n):
                act.wait_ge(sem["nmax1"], n)
                for g in range(G):
                    p = act.activation(p1[:, g, :], em[:, g, :], ACT.Exp, bias=nmax1[:, g:g + 1],
                                       accum_out=den1[:, g:g + 1])
                p.then_inc(sem["p1"], 1)

            def f_scaled(n):
                act.wait_ge(sem["rden1"], n)
                for g in range(G):
                    w = act.activation(whs[:, g, :], f[:, 2 + g, 0:D], ACT.Copy, scale=rden1[:, g:g + 1])
                w.then_inc(sem["whs"], 1)

            def f_elu(n):
                act.wait_ge(sem["mn"], n)
                act.activation(ex[:, :, :], mn[:, :, :], ACT.Exp).then_inc(sem["ex"], 1)

            def f_zt(n):
                act.wait_ge(sem["ZT"], n)
                copy(zt_hi[:, :, :], f[:, 1, :]).then_inc(sem["zt_hi"], 1)

            def f_exp_adj(n):
                act.wait_ge(sem["adjs"], n)
                act.activation(ed[:, :, :], adjs[:, :, :], ACT.Exp, scale=-1.0).then_inc(sem["ed"], 1)

            def s_relu(made, bank, bias, done, n):
                act.wait_ge(sem[made], n)
                for tile in (y_hi, y):
                    for c in range(C):
                        r = act.activation(tile[:, c, :], bank[:, c * G * N:(c + 1) * G * N], ACT.Relu, bias=bias[:, c:c + 1])
                        if tile is y:
                            r.then_inc(sem[done], 1)
                    if tile is y_hi:
                        r.then_inc(sem[f"{done}_hi"], 1)

            def s_sup(made, bank, done, n):
                act.wait_ge(sem[made], n)
                copy(sup[:, :, :], s_banks[:, bank, :]).then_inc(sem[done], 1)

            def s_h3(n):
                act.wait_ge(sem["T_h3"], n)
                for c in range(C):
                    act.activation(h3_hi[:, c, :, :], s_banks[:, 2, c * G * N:(c + 1) * G * N], ACT.Relu)\
                        .then_inc(sem["h3_hi"], 1)

            def s_q(n):
                act.wait_ge(sem["Q"], n)
                act.activation(qT[:, :, :, :], s_banks[:, 0:2, :], ACT.Copy, scale=SCALE).then_inc(sem["q"], 1)

            def s_k_even(n):
                act.wait_ge(sem["K"], n)
                copy(kbd[0:DH, :, :, 0, :], s_banks[0:DH, 2:4, :].rearrange("p b (q n) -> p (b q) n", n=N))\
                    .then_inc(sem["k_even"], 1)

            def s_v(n):
                act.wait_ge(sem["V"], n)
                copy(v[:, :, :], s_banks[:, 0:2, :]).then_inc(sem["v"], 1)

            def s_exps(q, n):
                act.wait_ge(sem[f"nm{q}"], n)
                for i in range(HALF):
                    e = act.activation(half(pr, q)[:, i, :], s_banks[:, BANKS[q], i * N:(i + 1) * N], ACT.Exp,
                                       bias=half(nm, q)[:, i:i + 1], accum_out=half(rs, q)[:, i:i + 1])
                e.then_inc(sem[f"pr{q}"], 1)

            def s_ot(g, n):
                act.wait_ge(sem[f"PV{g}"], n)
                copy(ot_hi[:, g, :, :], s_banks[:, BANKS[2 * g], :]).then_inc(sem[f"ot{g}_hi"], 1)

            def turn(f0, f1, s):
                if f0 is not None:
                    f_h0(f0)
                if s is not None:
                    s_sup("SA", 2, "supa", s)
                if f0 is not None:
                    f_x_copy(f0, f1)
                if s is not None:
                    s_relu("Y2", s_banks[:, 3, :], gb2, "y2", s)
                if f0 is not None:
                    f_s2(f0)
                if s is not None:
                    s_sup("SB", 1, "supb", s)
                if f1 is not None:
                    f_h1(f1)
                if s is not None:
                    s_h3(s)
                if f0 is not None:
                    f_exp0(f0)
                if f1 is not None:
                    f_exp_adj(f1)
                if s is not None:
                    s_q(s)
                if f1 is not None:
                    f_att1(f1)
                    f_scaled(f1)
                if s is not None:
                    s_k_even(s)
                if f1 is not None:
                    f_elu(f1)
                if s is not None:
                    s_v(s)
                if f0 is not None:
                    f_adj(f0, f1)
                if s is not None:
                    s_exps(0, s)
                if f0 is not None:
                    f_trT(f0)
                if s is not None:
                    s_exps(1, s)
                    s_exps(2, s)
                    s_exps(3, s)
                if f1 is not None:
                    f_zt(f1)
                if f0 is not None:
                    f_s1(f0)
                if s is not None:
                    s_ot(0, s)
                if f1 is not None:
                    s_relu("Y1", f[:, 3, :], gb1, "y1", f1)
                if s is not None:
                    s_ot(1, s)

            turn(1, None, None)
            act.wait_ge(sem["w_in3"], 16 * LOADS3)
            turn(2, 1, None)
            with act.Fori(1, PAIRS - 1) as t:
                turn(t + 2, t + 1, t)
            turn(None, PAIRS, PAIRS - 1)
            turn(None, None, PAIRS)

        @block.vector
        def _(dve):
            def hi_part(hi, full):
                return dve.tensor_copy(hi, full)

            def lo_part(lo, full, hi):
                return dve.tensor_tensor(lo, full, hi.bitcast(fp32), ALU.subtract)

            def norm_stats(k, src, n, by_graph=None):
                for g in range(G):
                    if by_graph is not None:
                        dve.wait_ge(by_graph, n * G - (G - 1 - g))
                    b = dve.bn_stats(stats[k][:, g, :], src[:, g, :])
                b.then_inc(sem[f"stats{k}"], 1)
                dve.wait_ge(sem[f"stats{k}"], n)
                dve.memset(spare[:, :], 0.0)
                for g in range(G):
                    b = dve.bn_aggr(mv[k][:, g, :], stats[k][:, g, :])
                b.then_inc(sem[f"mv{k}"], 1)
                dve.wait_ge(sem[f"mv{k}"], n)
                dve.tensor_scalar(veps[k][:, :], mv[k][:, :, 1], EPS, None, ALU.add).then_inc(sem[f"veps{k}"], 1)

            def norm_apply(k, src, n):
                dve.wait_ge(sem[f"rstd{k}"], n)
                for g in range(G):
                    dve.tensor_scalar(hn[k][:, g, :], src[:, g, :], mv[k][:, g, 0:1], rstd[k][:, g:g + 1],
                                      ALU.subtract, ALU.mult).then_inc(sem[f"hn{k}"], 1)

            def lo_relu(k, bank, hi, lo, n):
                dve.wait_ge(sem[f"h{k}_hi"], n * C if k == 3 else n)
                dve.scalar_tensor_tensor(lo[:, :, :, :].rearrange("p c g n -> p (c g n)"), bank, 0.0,
                                         hi[:, :, :, :].bitcast(fp32).rearrange("p c g n -> p (c g n)"),
                                         ALU.max, ALU.subtract).then_inc(sem[f"h{k}_lo"], 1)

            def f_norm0(n):
                dve.wait_ge(sem["x_in"], 16 * n)
                norm_stats(0, x0, n)

            def f_si(n):
                dve.wait_ge(sem["s2"], n)
                dve.tensor_scalar(sic[:, :], s2[:, :, D], c0[:, 0:1], None, ALU.add).then_inc(sem["si"], 1)

            def f_logits0(n):
                dve.wait_ge(sem["E0"], n)
                dve.wait_ge(sem["si"], n)
                for g in range(G):
                    z = dve.tensor_scalar(z0[:, g, :], s_banks[:, 3, g * N:(g + 1) * N], sic[:, g:g + 1], None, ALU.add)
                z.then_inc(sem["z0"], 1)

            def f_leaky0(n):
                dve.wait_ge(sem["z0"], n)
                dve.scalar_tensor_tensor(l0[:, :, :], z0[:, :, :], SLOPE, z0[:, :, :], ALU.mult, ALU.max)\
                    .then_inc(sem["l0"], 1)

            def f_transition(n):
                dve.wait_ge(sem["e0"], n)
                dve.wait_ge(sem["adj_in"], 16 * n)
                for g in range(G):
                    a = dve.tensor_tensor_reduce(out=alpha[:, g, :], in0=e0[:, g, :], in1=adj_ij[:, g, :], scale=1.0,
                                                 scalar=0.0, op0=ALU.mult, op1=ALU.add, accum_out=rsum[:, g:g + 1])
                a.then_inc(sem["alpha"], 1)
                dve.wait_ge(sem["alpha"], n)
                dve.tensor_scalar(rsume[:, :], rsum[:, :], ROW_EPS, None, ALU.add).then_inc(sem["rsume"], 1)
                dve.wait_ge(sem["rsume"], n)
                dve.reciprocal(rinv[:, :], rsume[:, :]).then_inc(sem["rinv"], 1)
                dve.wait_ge(sem["rinv"], n)
                for g in range(G):
                    a = dve.tensor_scalar(tr[:, g, :], alpha[:, g, :], rinv[:, g:g + 1], None, ALU.mult)
                a.then_inc(sem["tr"], 1)

            def f_xt(n):
                dve.wait_ge(sem["B0"], n)
                dve.tensor_tensor(xt[:, :, :], f[:, 2, :].rearrange("p (g d) -> p g d", g=G), per_graph(bsum), ALU.add)\
                    .then_inc(sem["xt"], 1)

            def f_x1(n):
                dve.wait_ge(sem["xt"], n)
                dve.wait_ge(sem["xr"], n)
                dve.scalar_tensor_tensor(x1[:, :, :], xt[:, :, :], 0.0, xr[:, :, :], ALU.max, ALU.add)\
                    .then_inc(sem["x1"], 1)

            def f_cap(n):
                dve.wait_ge(sem["adjT"], n)
                dve.tensor_scalar(cap[:, :, :], adj_ji[:, :, :], 0.5, CAP, ALU.is_gt, ALU.mult).then_inc(sem["cap"], 1)

            def f_parts1(n):
                dve.wait_ge(sem["Wh"], n)
                dve.tensor_copy(wh2[:, :, :], f[:, 2:4, D:EXT]).then_inc(sem["wh2"], 1)

            def f_logits1(n):
                dve.wait_ge(sem["E1"], n)
                for g in range(G):
                    z = dve.tensor_scalar(z1[:, g, :], f[:, 1, g * N:(g + 1) * N], wh2[:, g, 0:1], None, ALU.add)
                z.then_inc(sem["z1"], 1)

            def f_maxima1(n):
                dve.wait_ge(sem["z1"], n)
                dve.scalar_tensor_tensor(l1[:, :, :], z1[:, :, :], SLOPE, z1[:, :, :], ALU.mult, ALU.max)\
                    .then_inc(sem["l1"], 1)
                dve.wait_ge(sem["l1"], n)
                dve.wait_ge(sem["cap"], n)
                dve.scalar_tensor_tensor(em[:, :, :], cap[:, :, :], NEG_INF, l1[:, :, :], ALU.add, ALU.min)\
                    .then_inc(sem["em"], 1)
                dve.wait_ge(sem["em"], n)
                dve.tensor_reduce(nmax1[:, :], em[:, :, :], AX.X, ALU.max, negate=True).then_inc(sem["nmax1"], 1)

            def f_rden(n):
                dve.wait_ge(sem["p1"], n)
                dve.reciprocal(rden1[:, :], den1[:, :]).then_inc(sem["rden1"], 1)

            def f_x2(n):
                dve.wait_ge(sem["Hp"], n)
                dve.tensor_scalar(mn[:, :, :], f[:, 2, :].rearrange("p (g d) -> p g d", g=G), 0.0, None, ALU.min)\
                    .then_inc(sem["mn"], 1)
                dve.scalar_tensor_tensor(rx[:, :, :], f[:, 2, :].rearrange("p (g d) -> p g d", g=G), 0.0, x1[:, :, :],
                                         ALU.max, ALU.add).then_inc(sem["rx"], 1)

            def f_x2_sum(n):
                dve.wait_ge(sem["rx"], n)
                dve.wait_ge(sem["ex"], n)
                dve.scalar_tensor_tensor(x2[:, :, :], ex[:, :, :], -1.0, rx[:, :, :], ALU.add, ALU.add)\
                    .then_inc(sem["x2"], 1)

            def f_h2(n):
                dve.wait_ge(sem["hn2"], n * G)
                dve.tensor_scalar(h2[:, :, :], hn[2][:, :, :], 0.0, None, ALU.max).then_inc(sem["h2"], 1)

            def f_mask(n):
                dve.wait_ge(sem["mask_in"], 16 * n)
                m = mask_u8[:, :].rearrange("a (g n) -> a g n", g=G)
                dve.tensor_copy(mrow[0:1, :, :], m)
                dve.tensor_copy(mrow0[0:1, :, :], m)
                dve.tensor_scalar(mbig[0:1, :, :], m, BIG, None, ALU.mult).then_inc(sem["mrow"], 1)

            def s_bT(n):
                dve.wait_ge(sem["MM"], n)
                dve.wait_ge(sem["bd"], n)
                dve.tensor_tensor(bT[:, :, :], bd[:, :, :], f[:, 1, 0:G * N].rearrange("p (g n) -> p g n", g=G),
                                  ALU.mult).then_inc(sem["bT"], 1)

            def s_x3(n):
                dve.wait_ge(sem["x2b"], n)
                for g in range(G):
                    dve.wait_ge(sem["OUT"], n * G - (G - 1 - g))
                    dve.tensor_tensor(x3[:, g, :], s_banks[:, g, 0:D], x2b[:, g, :], ALU.add)\
                        .then_inc(sem["x3"], 1)

            def s_k_odd(n):
                dve.wait_ge(sem["K"], n)
                dve.tensor_copy(kbd[DH:P, :, :, 1, :], s_banks[DH:P, 2:4, :].rearrange("p b (q n) -> p (b q) n", n=N))\
                    .then_inc(sem["k_odd"], 1)

            def s_max(q, n):
                dve.wait_ge(sem[f"dots{q}"], n)
                dve.tensor_reduce(half(nm, q), s_banks[:, BANKS[q], :].rearrange("p (h n) -> p h n", n=N),
                                  AX.X, ALU.max, negate=True).then_inc(sem[f"nm{q}"], 1)

            def s_rsum(q, n):
                dve.wait_ge(sem[f"pr{q}"], n)
                dve.reciprocal(half(ri, q), half(rs, q)).then_inc(sem[f"ri{q}"], 1)

            def s_at(q, n):
                dve.wait_ge(sem[f"PT{q}"], n)
                dve.tensor_tensor(half(at, q), s_banks[:, BANKS[q], :].rearrange("p (h n) -> p h n", n=N),
                                  bT[:, q // 2, :].unsqueeze(1).broadcast_to([P, HALF, N]), ALU.add).then_inc(sem[f"at{q}"], 1)

            def s_y_lo(layer, n):
                for c in range(C):
                    dve.wait_ge(sem[f"y{layer}"], n * C - (C - 1 - c))
                    last = dve.tensor_tensor(y_lo[:, c, :], y[:, c, :], y_hi[:, c, :].bitcast(fp32), ALU.subtract)
                last.then_inc(sem[f"y{layer}_lo"], 1)

            def f_zt_lo(n):
                dve.wait_ge(sem["zt_hi"], n)
                dve.tensor_tensor(zt_lo[:, :, :].rearrange("p c n -> p (c n)"), f[:, 1, :],
                                  zt_hi[:, :, :].bitcast(fp32).rearrange("p c n -> p (c n)"), ALU.subtract)\
                    .then_inc(sem["zt_lo"], 1)

            def s_ot_lo(g, n):
                dve.wait_ge(sem[f"ot{g}_hi"], n)
                dve.tensor_tensor(ot_lo[:, g, :, :].rearrange("p h n -> p (h n)"), s_banks[:, BANKS[2 * g], :],
                                  ot_hi[:, g, :, :].bitcast(fp32).rearrange("p h n -> p (h n)"), ALU.subtract)\
                    .then_inc(sem[f"ot{g}_lo"], 1)

            def s_x4(g, n):
                dve.wait_ge(sem[f"W{g}"], n)
                if g == 0:
                    dve.wait_ge(sem["x3b"], n)
                    dve.wait_ge(sem["out_done"], 16 * n)
                projected = s_banks[:, 1, 0:D] if g == 0 else s_banks[:, 3, D:2 * D]
                dve.scalar_tensor_tensor(x4[:, g, :], projected, LA, x3b[:, g, :], ALU.mult, ALU.add)\
                    .then_inc(sem[f"x4_{g}"], 1)

            def turn(fn, f0, f1, s, so, after_h0=None, after_rden=None):
                if f0 is not None:
                    lo_relu(0, f[:, 0, :], h0_hi, h0_lo, f0)
                if after_h0 is not None:
                    after_h0()
                if f1 is not None:
                    dve.wait_ge(sem["x1"], f1)
                    norm_stats(1, x1, f1)
                if s is not None:
                    s_bT(s)
                if so is not None:
                    s_x4(0, so)
                if f1 is not None:
                    norm_apply(1, x1, f1)
                if s is not None:
                    s_y_lo(2, s)
                if f0 is not None:
                    f_si(f0)
                    f_logits0(f0)
                if s is not None:
                    s_x3(s)
                    norm_stats(3, x3, s, sem["x3"])
                if f1 is not None:
                    lo_relu(1, s_banks[:, 2, :], h1_hi, h1_lo, f1)
                if s is not None:
                    norm_apply(3, x3, s)
                if so is not None:
                    s_x4(1, so)
                if f0 is not None:
                    f_leaky0(f0)
                if f1 is not None:
                    f_parts1(f1)
                if s is not None:
                    lo_relu(3, s_banks[:, 2, :], h3_hi, h3_lo, s)
                if f1 is not None:
                    f_logits1(f1)
                    f_maxima1(f1)
                if f0 is not None:
                    f_transition(f0)
                if f1 is not None:
                    f_rden(f1)
                if after_rden is not None:
                    after_rden()
                if s is not None:
                    s_k_odd(s)
                if f1 is not None:
                    f_x2(f1)
                    f_x2_sum(f1)
                    dve.wait_ge(sem["x2"], f1)
                    norm_stats(2, x2, f1)
                if s is not None:
                    s_max(0, s)
                    s_max(1, s)
                if f1 is not None:
                    norm_apply(2, x2, f1)
                if f0 is not None:
                    f_cap(f0)
                if s is not None:
                    s_rsum(0, s)
                if f1 is not None:
                    f_h2(f1)
                if s is not None:
                    s_max(2, s)
                    s_rsum(1, s)
                    s_max(3, s)
                    s_at(0, s)
                    s_rsum(2, s)
                if f1 is not None:
                    f_mask(f1)
                if s is not None:
                    s_at(1, s)
                    s_rsum(3, s)
                if f1 is not None:
                    f_zt_lo(f1)
                if fn is not None:
                    f_norm0(fn)
                if s is not None:
                    s_at(2, s)
                    s_at(3, s)
                    s_ot_lo(0, s)
                if fn is not None:
                    norm_apply(0, x0, fn)
                if f1 is not None:
                    s_y_lo(1, f1)
                if f0 is not None:
                    f_xt(f0)
                    f_x1(f0)
                if s is not None:
                    s_ot_lo(1, s)

            turn(1, None, None, None, None)
            dve.wait_ge(sem["w_in"], 16 * LOADS1)
            wl1 = w_raw[:, :, 3 * D:4 * D]
            k = 0
            for c in range(C):
                for j in range(2):
                    dve.tensor_tensor_reduce(out=products[:, k, :], in0=wv_raw[:, c, :], in1=aw_bc[:, j, :], scale=1.0,
                                             scalar=0.0, op0=ALU.mult, op1=ALU.add, accum_out=att0[:, c, j:j + 1])
                    dve.tensor_tensor_reduce(out=products[:, k + 1, :], in0=wl1[:, c, :], in1=a_bc[:, j, :], scale=1.0,
                                             scalar=0.0, op0=ALU.mult, op1=ALU.add, accum_out=att1[:, c, j:j + 1])
                    k += 2
            for j in range(2):
                last = dve.tensor_tensor_reduce(out=products[:, k + j, :], in0=bv_bc[:, :], in1=aw_bc[:, j, :], scale=1.0,
                                                scalar=0.0, op0=ALU.mult, op1=ALU.add, accum_out=c_part[:, j:j + 1])
            last.then_inc(sem["w_att"], 1)
            dve.wait_ge(sem["w_att"], 1)
            dve.tensor_tensor(c_part[:, 2:3], c_part[:, 0:1], c_part[:, 1:2], ALU.add).then_inc(sem["w_c"], 1)
            dve.tensor_tensor(bsum_a[:, :], bk_bc[:, 0, :], bk_bc[:, 1, :], ALU.add).then_inc(sem["w_bsum"], 1)
            dve.wait_ge(sem["w_c"], 1)
            dve.tensor_tensor(c0[:, :], c_part[:, 2:3], ab_bc[:, :], ALU.add)
            dve.wait_ge(sem["w_bsum"], 1)
            dve.tensor_tensor(bsum[:, :], bsum_a[:, :], bk_bc[:, 2, :], ALU.add)
            cols0 = [(k_hi[:, :, j, 0:D], k_lo[:, :, j, 0:D], w_raw[:, :, j * D:(j + 1) * D]) for j in range(KHOPS)]
            cols1 = [(k_hi[:, :, KHOPS - 1, D + i:D + i + 1], k_lo[:, :, KHOPS - 1, D + i:D + i + 1], att0[:, :, 1 - i:2 - i])
                     for i in range(2)]
            cols2 = [(w1_hi[:, :, 0:D], w1_lo[:, :, 0:D], wl1)]
            cols3 = [(w1_hi[:, :, D + i:D + i + 1], w1_lo[:, :, D + i:D + i + 1], att1[:, :, 1 - i:2 - i]) for i in range(2)]
            parts = cols0 + cols1 + cols2 + cols3
            for hi, lo, full in parts:
                last = hi_part(hi, full)
            last.then_inc(sem["w_hi"], 1)
            dve.wait_ge(sem["w_hi"], 1)
            for hi, lo, full in parts:
                last = lo_part(lo, full, hi)
            last.then_inc(sem["w_split"], 1)

            def split_layer2():
                dve.memset(mrow0[:, :, :], 0.0)
                dve.memset(mrow[:, :, :], 0.0)
                dve.memset(mbig[:, :, :], 0.0).then_inc(sem["mask_pad"], 1)
                dve.wait_ge(sem["mask_pad"], 1)
                dve.memset(mrow[0:2, :, :], 1.0)
                dve.memset(mbig[0:2, :, :], -BIG).then_inc(sem["mask_pad"], 1)
                dve.wait_ge(sem["w_in3"], 16 * LOADS3)
                for hi, full in ((g1_hi, g1), (g2_hi, g2), (g3_hi, g3)):
                    hi_part(hi[:, :, :], full[:, :, :])
                hi_part(wout_hi[:, :, :], wout[:, :, :]).then_inc(sem["w_hi"], 1)
                dve.wait_ge(sem["w_hi"], 2)
                for lo, full, hi in ((g1_lo, g1, g1_hi), (g2_lo, g2, g2_hi), (g3_lo, g3, g3_hi)):
                    lo_part(lo[:, :, :], full[:, :, :], hi[:, :, :])
                lo_part(wout_lo[:, :, :], wout[:, :, :], wout_hi[:, :, :]).then_inc(sem["w_split2"], 1)

            def split_qkv():
                dve.wait_ge(sem["w_in2"], 16 * LOADS2)
                hi_part(qkv_hi[:, :, :], w_raw[:, :, :]).then_inc(sem["w_hi"], 1)
                dve.wait_ge(sem["w_hi"], 3)
                lo_part(qkv_lo[:, :, :], w_raw[:, :, :], qkv_hi[:, :, :]).then_inc(sem["w_split3"], 1)

            turn(2, 1, None, None, None, after_h0=split_layer2)
            dve.wait_ge(sem["mask_pad"], 2)
            turn(3, 2, 1, None, None, after_rden=split_qkv)
            turn(4, 3, 2, 1, None)
            with dve.Fori(2, PAIRS - 2) as t:
                turn(t + 3, t + 2, t + 1, t, t - 1)
            turn(None, PAIRS, PAIRS - 1, PAIRS - 2, PAIRS - 3)
            turn(None, None, PAIRS, PAIRS - 1, PAIRS - 2)
            turn(None, None, None, PAIRS, PAIRS - 1)
            turn(None, None, None, None, PAIRS)

        @block.tensor
        def _(pe):
            def mm(o, lhsT, rhs, start=True, stop=True, **kw):
                return pe.matmul(o, lhsT, rhs, start=start, stop=stop, **kw)

            def chunks3(o, pairs, start=True, stop=True, **kw):
                for i, (lh, ll, rh, rl) in enumerate(pairs):
                    mm(o, ll, rh, start=start and i == 0, stop=False, **kw)
                    mm(o, lh, rl, start=False, stop=False, **kw)
                    last = mm(o, lh, rh, start=False, stop=stop and i == len(pairs) - 1, **kw)
                return last

            def transposes(bank, k, n):
                for g in range(G):
                    pe.wait_ge(sem[f"hn{k}"], n * G - (G - 1 - g))
                    for c in range(C):
                        o = (c * G + g) * N
                        last = pe.transpose(bank[:, o:o + N], hn[k][:, g, c * P:(c + 1) * P], ident[:, :])
                return last

            def hi_first(banks, by_chunk=None):
                for c in range(C):
                    if by_chunk is not None:
                        by_chunk(c)
                    for bank in banks:
                        for r, (o, early, _) in enumerate(bank):
                            for i in range(2):
                                mm(o, *early[c * 2 + i], start=(c == 0 and r == 0 and i == 0), stop=False,
                                   skip_group_check=True)

            def lo_last(banks):
                for bank in banks:
                    for o, _, late in bank:
                        for a, b in late:
                            last = mm(o, a, b, start=False, skip_group_check=True)
                return last

            def as_moving(o, w_hi, w_lo, h_hi, h_lo):
                early = [(w(c), h_hi[:, c, :, :]) for c in range(C) for w in (w_lo, w_hi)]
                return o, early, [(w_hi(c), h_lo[:, c, :, :]) for c in range(C)]

            def as_stationary(o, g, h_hi, h_lo, w_hi, w_lo):
                early = [(h_hi[:, c, g, :], w(c)) for c in range(C) for w in (w_lo, w_hi)]
                return o, early, [(h_lo[:, c, g, :], w_hi(c)) for c in range(C)]

            def by_node(hi, lo, g, w_hi, w_lo):
                return [(hi[:, c, g, :], lo[:, c, g, :], w_hi(c), w_lo(c)) for c in range(C)]

            def f_transpose0(n, f1):
                if f1 is not None:
                    pe.wait_ge(sem["s1"], f1)
                transposes(f[:, 0, :], 0, n).then_inc(sem["T_h0"], 1)

            def f_transpose_adj(n, f1):
                pe.wait_ge(sem["adj_in"], 16 * n)
                if f1 is not None:
                    pe.wait_ge(sem["z1"], f1)
                for g in range(G):
                    last = pe.transpose(f[:, 1, g * N:(g + 1) * N], adj_ij[:, g, :], ident[:, :])
                last.then_inc(sem["T_adj"], 1)

            def f_logits0(n):
                pe.wait_ge(sem["s2"], n)
                for g in range(G):
                    last = pe.transpose(s_banks[:, 3, g * N:(g + 1) * N], s2[:, g, D + 1:EXT].broadcast_to([P, N]), ident[:, :])
                last.then_inc(sem["E0"], 1)

            def f_hop2(n, f1):
                pe.wait_ge(sem["h0_lo"], n)
                if f1 is not None:
                    pe.wait_ge(sem["xt"], f1)
                for g in range(G):
                    last = chunks3(f[:, 2 + g, 0:EXT], by_node(h0_hi, h0_lo, g, lambda c: k_hi[:, c, KHOPS - 1, :],
                                                               lambda c: k_lo[:, c, KHOPS - 1, :]))
                last.then_inc(sem["S2p"], 1)

            def f_hop1(n, f1):
                pe.wait_ge(sem["h0_lo"], n)
                for g in range(G):
                    chunks3(f[:, 0, g * D:(g + 1) * D], by_node(h0_hi, h0_lo, g, lambda c: k_hi[:, c, 1, 0:D],
                                                                lambda c: k_lo[:, c, 1, 0:D]),
                            start=(g == 0), stop=False, skip_group_check=True)

            def f_trT(n):
                pe.wait_ge(sem["tr"], n)
                pe.wait_ge(sem["adjT"], n)
                for g in range(G):
                    last = pe.transpose(f[:, 1, g * N:(g + 1) * N], tr[:, g, :], ident[:, :])
                last.then_inc(sem["TT"], 1)

            def f_aggregate(bank, src, made, done, n):
                pe.wait_ge(sem["trT"], n)
                pe.wait_ge(sem[made], n)
                for g in range(G):
                    last = mm(f[:, bank, g * D:(g + 1) * D], trT[:, g, :], src[:, g, 0:D], start=False,
                              skip_group_check=True)
                last.then_inc(sem[done], 1)

            def f_hop0(n, f1):
                if f1 is not None:
                    pe.wait_ge(sem["rx"], f1)
                for g in range(G):
                    chunks3(f[:, 2, g * D:(g + 1) * D], by_node(h0_hi, h0_lo, g, lambda c: k_hi[:, c, 0, 0:D],
                                                                lambda c: k_lo[:, c, 0, 0:D]),
                            start=(g == 0), stop=False, skip_group_check=True)

            def f_transpose1(n):
                transposes(s_banks[:, 2, :], 1, n).then_inc(sem["T_h1"], 1)

            def f_products1(g, n, f0):
                pe.wait_ge(sem["h1_lo"], n)
                if f0 is not None:
                    pe.wait_ge(sem["s2"], f0)
                last = chunks3(f[:, 2 + g, 0:EXT], by_node(h1_hi, h1_lo, g, lambda c: w1_hi[:, c, :],
                                                           lambda c: w1_lo[:, c, :]))
                if g == G - 1:
                    last.then_inc(sem["Wh"], 1)

            def f_logits1(n, s):
                pe.wait_ge(sem["wh2"], n)
                if s is not None:
                    pe.wait_ge(sem["bT"], s)
                for g in range(G):
                    last = pe.transpose(f[:, 1, g * N:(g + 1) * N], wh2[:, g, 1:2].broadcast_to([P, N]), ident[:, :])
                last.then_inc(sem["E1"], 1)

            def f_attend1(n):
                pe.wait_ge(sem["whs"], n)
                for g in range(G):
                    last = mm(f[:, 2, g * D:(g + 1) * D], p1[:, g, :], whs[:, g, :])
                last.then_inc(sem["Hp"], 1)

            def f_aggregate_h(n):
                pe.wait_ge(sem["h2"], n)
                pe.wait_ge(sem["adjs"], n)
                for c in range(C):
                    for g in range(G):
                        o = (c * G + g) * N
                        last = mm(f[:, 1, o:o + N], h2[:, g, c * P:(c + 1) * P], adjs[:, g, :])
                last.then_inc(sem["ZT"], 1)

            def s_mask(n):
                pe.wait_ge(sem["mrow"], n)
                for g in range(G):
                    last = mm(f[:, 1, g * N:(g + 1) * N], mrow0[:, g, :], mrow0[:, g, :])
                last.then_inc(sem["MM"], 1)

            def s_first(n):
                pe.wait_ge(sem["zt_lo"], n)
                for o in range(C):
                    cols = slice(o * P, (o + 1) * P)
                    last = chunks3(f[:, 3, o * G * N:(o + 1) * G * N],
                                   [(g1_hi[:, c, cols], g1_lo[:, c, cols], zt_hi[:, c, :], zt_lo[:, c, :]) for c in range(C)])
                last.then_inc(sem["Y1"], 1)

            def s_support(bank, w_hi, w_lo):
                return [[as_stationary(s_banks[:, bank, g * D:(g + 1) * D], g, y_hi[:, :, :].rearrange("p c (g n) -> p c g n", g=G),
                                       y_lo[:, :, :].rearrange("p c (g n) -> p c g n", g=G),
                                       lambda c: w_hi[:, c, :], lambda c: w_lo[:, c, :]) for g in range(G)]]

            def s_support_a(n):
                a = s_support(2, g2_hi, g2_lo)
                pe.wait_ge(sem["y1_lo"], n)
                hi_first(a)
                lo_last(a).then_inc(sem["SA"], 1)

            def s_support_b(n, so):
                pe.wait_ge(sem["y2_hi"], n)
                if so is not None:
                    pe.wait_ge(sem["x4_0"], so)
                b = s_support(1, g3_hi, g3_lo)
                hi_first(b)
                pe.wait_ge(sem["y2_lo"], n)
                lo_last(b).then_inc(sem["SB"], 1)

            def s_second(n):
                pe.wait_ge(sem["supa"], n)
                for o in range(C):
                    for g in range(G):
                        a = (o * G + g) * N
                        last = mm(s_banks[:, 3, a:a + N], sup[:, g, o * P:(o + 1) * P], adjs[:, g, :])
                last.then_inc(sem["Y2"], 1)

            def s_third(n):
                pe.wait_ge(sem["supb"], n)
                for g in range(G):
                    mm(s_banks[:, g, 0:D], adjs[:, g, :], sup[:, g, :]).then_inc(sem["OUT"], 1)

            def s_transpose3(n, f1):
                if f1 is not None:
                    pe.wait_ge(sem["h1_lo"], f1)
                transposes(s_banks[:, 2, :], 3, n).then_inc(sem["T_h3"], 1)

            def s_heads(kind, bank):
                def region(hp):
                    a = kind * INNER + hp * P
                    return as_moving(s_banks[:, bank + hp // 2, (hp % 2) * G * N:(hp % 2 + 1) * G * N],
                                     lambda c: qkv_hi[:, c, a:a + P], lambda c: qkv_lo[:, c, a:a + P], h3_hi, h3_lo)
                return [[region(hp) for hp in range(b * HP // 2, (b + 1) * HP // 2)] for b in range(2)]

            def s_queries_hi(n):
                q = s_heads(0, 0)
                hi_first(q, lambda c: pe.wait_ge(sem["h3_hi"], n * C - (C - 1 - c)))

            def s_queries_lo(n):
                q = s_heads(0, 0)
                pe.wait_ge(sem["h3_lo"], n)
                lo_last(q).then_inc(sem["Q"], 1)

            def s_keys(n, f0, so):
                if so is not None:
                    pe.wait_ge(sem["x4_1"], so)
                if f0 is not None:
                    pe.wait_ge(sem["z0"], f0)
                k = s_heads(1, 2)
                hi_first(k)
                lo_last(k).then_inc(sem["K"], 1)

            def s_values(g, n):
                pe.wait_ge(sem["q"], n)
                a = 2 * INNER
                last = chunks3(s_banks[:, g, :], by_node(h3_hi, h3_lo, g, lambda c: qkv_hi[:, c, a:a + INNER],
                                                         lambda c: qkv_lo[:, c, a:a + INNER]))
                if g == G - 1:
                    last.then_inc(sem["V"], 1)

            def s_dots(q, n):
                if q == 0:
                    pe.wait_ge(sem["k_even"], n)
                    pe.wait_ge(sem["k_odd"], n)
                if q == 2:
                    pe.wait_ge(sem["v"], n)
                g, bank = q // 2, s_banks[:, BANKS[q], :]
                mm(bank, mrow[:, g, :], mbig[:, g, :].unsqueeze(1).broadcast_to([P, HALF, N]), stop=False,
                   skip_group_check=True)
                for i in range(2):
                    hp = 2 * (q % 2) + i
                    last = mm(bank[:, i * 2 * N:(i + 1) * 2 * N], qT[:, hp, g, :], kbd[:, hp, g, :, :], start=False,
                              skip_group_check=True)
                last.then_inc(sem[f"dots{q}"], 1)

            def s_transpose_p(q, n):
                pe.wait_ge(sem[f"pn{q}"], n)
                for i in range(HALF):
                    last = pe.transpose(s_banks[:, BANKS[q], i * N:(i + 1) * N], half(pn, q)[:, i, :], ident[:, :])
                last.then_inc(sem[f"PT{q}"], 1)

            def s_attend(q, n):
                g = q // 2
                pe.wait_ge(sem[f"at{q}"], n)
                for i in range(HALF):
                    h = HALF * (q % 2) + i
                    rows, hp = (h % 2) * DH, h // 2
                    last = mm(s_banks[rows:rows + DH, BANKS[2 * g], hp * N:(hp + 1) * N], v[:, g, h * DH:(h + 1) * DH],
                              at[:, g, h, :])
                if q % 2 == 1:
                    last.then_inc(sem[f"PV{g}"], 1)

            def s_project(g, n, part, free):
                if part == 0:
                    pe.wait_ge(sem[f"ot{g}_lo"], n)
                    if free is not None:
                        pe.wait_ge(*free)
                o = s_banks[:, 1, 0:D] if g == 0 else s_banks[:, 3, D:2 * D]
                last = chunks3(o, [(ot_hi[:, g, hp, :], ot_lo[:, g, hp, :], wout_hi[:, hp, :], wout_lo[:, hp, :])
                                   for hp in range(part * HP // 2, (part + 1) * HP // 2)],
                               start=(part == 0), stop=(part == 1), skip_group_check=True)
                if part == 1:
                    last.then_inc(sem[f"W{g}"], 1)

            def turn(f0, f1, s, so):
                if f0 is not None:
                    f_transpose0(f0, f1)
                if s is not None:
                    s_support_a(s)
                    s_mask(s)
                if so is not None:
                    s_project(0, so, 1, None)
                if s is not None:
                    s_second(s)
                if f0 is not None:
                    f_hop2(f0, f1)
                if s is not None:
                    s_support_b(s, so)
                if f1 is not None:
                    f_transpose1(f1)
                if f0 is not None:
                    f_logits0(f0)
                if s is not None:
                    s_third(s)
                if f0 is not None:
                    f_hop1(f0, f1)
                if so is not None:
                    s_project(1, so, 0, None if f0 is None else (sem["z0"], f0))
                    s_project(1, so, 1, None)
                if f1 is not None:
                    f_products1(0, f1, f0)
                if s is not None:
                    s_transpose3(s, f1)
                if f1 is not None:
                    f_products1(1, f1, f0)
                if s is not None:
                    s_queries_hi(s)
                if f1 is not None:
                    f_logits1(f1, s)
                if s is not None:
                    s_queries_lo(s)
                    s_keys(s, f0, so)
                    s_values(0, s)
                if f1 is not None:
                    f_attend1(f1)
                if s is not None:
                    s_values(1, s)
                if f0 is not None:
                    f_transpose_adj(f0, f1)
                if s is not None:
                    s_dots(0, s)
                    s_dots(1, s)
                if f0 is not None:
                    f_trT(f0)
                if s is not None:
                    s_dots(2, s)
                    s_dots(3, s)
                if f0 is not None:
                    f_aggregate(0, s2, "s2", "A0", f0)
                if s is not None:
                    s_transpose_p(0, s)
                if f0 is not None:
                    f_hop0(f0, f1)
                if s is not None:
                    s_transpose_p(1, s)
                if f1 is not None:
                    f_aggregate_h(f1)
                if s is not None:
                    s_attend(0, s)
                    s_transpose_p(2, s)
                    s_attend(1, s)
                    s_transpose_p(3, s)
                if f1 is not None:
                    s_first(f1)
                if f0 is not None:
                    f_aggregate(2, s1, "s1", "B0", f0)
                if s is not None:
                    s_attend(2, s)
                    s_project(0, s, 0, (sem["at3"], s))
                    s_attend(3, s)

            pe.wait_ge(sem["id_set"], 1)
            pe.wait_ge(sem["w_split"], 1)
            turn(1, None, None, None)
            pe.wait_ge(sem["w_split2"], 1)
            turn(2, 1, None, None)
            pe.wait_ge(sem["pad_set"], 1)
            pe.wait_ge(sem["w_split3"], 1)
            turn(3, 2, 1, None)
            with pe.Fori(2, PAIRS - 1) as t:
                turn(t + 2, t + 1, t, t - 1)
            turn(None, PAIRS, PAIRS - 1, PAIRS - 2)
            turn(None, None, PAIRS, PAIRS - 1)
            turn(None, None, None, PAIRS)


_INS = ["x", "adj", "nodemask", "L0_gnn_Wv", "L0_gnn_bv", "L0_gnn_aw", "L0_gnn_ab", "L0_gnn_Wk", "L0_gnn_bk",
        "L1_gnn_W", "L1_gnn_a", "L2_gnn_W1", "L2_gnn_b1", "L2_gnn_W2", "L2_gnn_b2", "L2_gnn_W3", "L2_gnn_b3",
        "L3_gnn_W_qkv", "L3_gnn_W_out", "L3_gnn_b_out"]


def kernel(**inputs):
    import numpy as _np
    import concourse.bacc as _bacc
    from concourse import mybir as _mybir
    from concourse.bass_utils import run_bass_kernel_spmd as _run

    nc = _bacc.Bacc("TRN2", target_bir_lowering=False, num_devices=1)
    arrays, args = {}, []
    for name in _INS:
        a = _np.ascontiguousarray(inputs[name])
        if a.dtype == bool:
            a = a.view(_np.uint8)
        arrays[f"in_{name}"] = a
        args.append(nc.dram_tensor(f"in_{name}", a.shape, _mybir.dt.from_np(a.dtype), kind="ExternalInput").ap())
    shape = inputs["x"].shape
    args.append(nc.dram_tensor("out_x", shape, _mybir.dt.float32, kind="ExternalOutput").ap())
    build(nc, *args)
    r = _run(nc, [arrays], core_ids=[0])
    return r.results[0]["out_x"]
```
